# Optimizing a Trainium2 kernel written in Bass

```python
import numpy as np
import jax
import jax.numpy as jnp

def _softmax(x, axis=-1):
    return jax.nn.softmax(x, axis=axis)

def _gelu(x):
    return jax.nn.gelu(x, approximate=True)

def _silu(x):
    return jax.nn.silu(x)

def _sigmoid(x):
    return jax.nn.sigmoid(x)

def _layernorm(x, axis=-1, eps=1e-05):
    m = jnp.mean(x, axis=axis, keepdims=True)
    v = jnp.var(x, axis=axis, keepdims=True)
    return (x - m) / jnp.sqrt(v + eps)

def _scatter_add(tgt, idx, src, axis=0):
    return tgt.at[idx].add(src)

def _segment_sum(src, seg, n):
    return jax.ops.segment_sum(src, seg, n)
kernel_name = 'mk_seq_preln_d1_jaxref_r8_f33dcc'

def setup_inputs(seed: int=0):
    np.random.seed(seed)
    _w = jnp.asarray

    def _L0_attn_setup():
        import jax, jax.numpy as jnp
        import numpy as np
        D_MODEL = 256
        N_HEADS = 16
        D_HEAD = D_MODEL // N_HEADS
        B, S = (2, 256)
        EPS = 1e-05

        def _mhsa(X, ln_g, ln_b, Wq, bq, Wk, bk, Wv, bv, Wo, bo):
            n_ctx = X.shape[-2]
            mu = jnp.mean(X, axis=-1, keepdims=True)
            var = jnp.mean(jnp.square(X - mu), axis=-1, keepdims=True)
            Xn = (X - mu) * jax.lax.rsqrt(var + EPS) * ln_g + ln_b

            def split_heads(t):
                return t.reshape(t.shape[:-1] + (N_HEADS, D_HEAD)).swapaxes(-2, -3)
            Q = split_heads(Xn @ Wq + bq)
            K = split_heads(Xn @ Wk + bk)
            V = split_heads(Xn @ Wv + bv)
            scores = jnp.einsum('bhqd,bhkd->bhqk', Q, K) / jnp.sqrt(jnp.float32(D_HEAD))
            causal = jnp.tril(jnp.ones((n_ctx, n_ctx), dtype=bool))
            scores = jnp.where(causal, scores, jnp.float32(-jnp.inf))
            A = jax.nn.softmax(scores, axis=-1)
            AV = jnp.einsum('bhqk,bhkd->bhqd', A, V)
            AV = AV.swapaxes(-2, -3).reshape(X.shape[:-1] + (D_MODEL,))
            return AV @ Wo + bo
        key = jax.random.key(seed)
        ks = jax.random.split(key, 10)
        sd = 1.0 / np.sqrt(D_MODEL)
        inp = {'X': jax.random.normal(ks[0], (B, S, D_MODEL), dtype=jnp.float32), 'ln_g': jnp.ones((D_MODEL,), jnp.float32), 'ln_b': jnp.zeros((D_MODEL,), jnp.float32), 'Wq': jax.random.uniform(ks[1], (D_MODEL, D_MODEL), jnp.float32, -sd, sd), 'bq': jax.random.uniform(ks[2], (D_MODEL,), jnp.float32, -sd, sd), 'Wk': jax.random.uniform(ks[3], (D_MODEL, D_MODEL), jnp.float32, -sd, sd), 'bk': jax.random.uniform(ks[4], (D_MODEL,), jnp.float32, -sd, sd), 'Wv': jax.random.uniform(ks[5], (D_MODEL, D_MODEL), jnp.float32, -sd, sd), 'bv': jax.random.uniform(ks[6], (D_MODEL,), jnp.float32, -sd, sd), 'Wo': jax.random.uniform(ks[7], (D_MODEL, D_MODEL), jnp.float32, -sd, sd), 'bo': jax.random.uniform(ks[8], (D_MODEL,), jnp.float32, -sd, sd)}
        return inp
    _L0_attn_in = _L0_attn_setup()

    def _L0_ffn_setup():
        import jax, jax.numpy as jnp
        import numpy as np
        HIDDEN = 256
        INTER = 1024
        SCALE = 64.0

        def fwht(x):
            orig_shape = x.shape
            n = orig_shape[-1]
            x = x.reshape(-1, n)
            h = 1
            while h < n:
                x = x.reshape(-1, n // (2 * h), 2, h)
                a, b = (x[:, :, 0, :], x[:, :, 1, :])
                x = jnp.stack([a + b, a - b], axis=2).reshape(-1, n)
                h *= 2
            return (x / jnp.sqrt(jnp.asarray(n, x.dtype))).reshape(orig_shape)
        key = jax.random.key(seed)
        ks = jax.random.split(key, 8)
        inp = jax.random.normal(ks[0], (4, 256, HIDDEN), dtype=jnp.float32)
        SU_ug = jnp.where(jax.random.bernoulli(ks[1], 0.5, (HIDDEN,)), 1.0, -1.0).astype(jnp.float32)
        SU_dp = jnp.where(jax.random.bernoulli(ks[2], 0.5, (INTER,)), 1.0, -1.0).astype(jnp.float32)
        Wscale_ug = jax.random.uniform(ks[3], (2 * INTER,), jnp.float32, 0.5, 1.5)
        Wscale_dp = jax.random.uniform(ks[4], (HIDDEN,), jnp.float32, 0.5, 1.5)
        W_up = jax.random.normal(ks[5], (INTER, HIDDEN), dtype=jnp.float32) * 0.02
        W_gate = jax.random.normal(ks[6], (INTER, HIDDEN), dtype=jnp.float32) * 0.02
        W_down = jax.random.normal(ks[7], (HIDDEN, INTER), dtype=jnp.float32) * 0.02
        return {'input': inp, 'SU_ug': SU_ug, 'SU_dp': SU_dp, 'Wscale_ug': Wscale_ug, 'Wscale_dp': Wscale_dp, 'W_up': W_up, 'W_gate': W_gate, 'W_down': W_down}
    _L0_ffn_in = _L0_ffn_setup()
    _d = {'L0_attn_X': _L0_attn_in['X'], 'L0_attn_ln_g': _L0_attn_in['ln_g'], 'L0_attn_ln_b': _L0_attn_in['ln_b'], 'L0_attn_Wq': _L0_attn_in['Wq'], 'L0_attn_bq': _L0_attn_in['bq'], 'L0_attn_Wk': _L0_attn_in['Wk'], 'L0_attn_bk': _L0_attn_in['bk'], 'L0_attn_Wv': _L0_attn_in['Wv'], 'L0_attn_bv': _L0_attn_in['bv'], 'L0_attn_Wo': _L0_attn_in['Wo'], 'L0_attn_bo': _L0_attn_in['bo'], 'L0_ffn_SU_ug': _L0_ffn_in['SU_ug'], 'L0_ffn_SU_dp': _L0_ffn_in['SU_dp'], 'L0_ffn_Wscale_ug': _L0_ffn_in['Wscale_ug'], 'L0_ffn_Wscale_dp': _L0_ffn_in['Wscale_dp'], 'L0_ffn_W_up': _L0_ffn_in['W_up'], 'L0_ffn_W_gate': _L0_ffn_in['W_gate'], 'L0_ffn_W_down': _L0_ffn_in['W_down']}
    _x0 = _d['L0_attn_X']
    _d['L0_attn_X'] = jax.random.normal(jax.random.fold_in(jax.random.key(seed), 1), (1, 2048, 256), dtype=_x0.dtype)
    del _x0
    return _d

def reference(L0_attn_X, L0_attn_ln_g, L0_attn_ln_b, L0_attn_Wq, L0_attn_bq, L0_attn_Wk, L0_attn_bk, L0_attn_Wv, L0_attn_bv, L0_attn_Wo, L0_attn_bo, L0_ffn_SU_ug, L0_ffn_SU_dp, L0_ffn_Wscale_ug, L0_ffn_Wscale_dp, L0_ffn_W_up, L0_ffn_W_gate, L0_ffn_W_down):

    def _L0_attn_ref(X, ln_g, ln_b, Wq, bq, Wk, bk, Wv, bv, Wo, bo):
        import jax, jax.numpy as jnp
        import numpy as np
        D_MODEL = 256
        N_HEADS = 16
        D_HEAD = D_MODEL // N_HEADS
        B, S = (2, 256)
        EPS = 1e-05

        def _mhsa(X, ln_g, ln_b, Wq, bq, Wk, bk, Wv, bv, Wo, bo):
            n_ctx = X.shape[-2]
            mu = jnp.mean(X, axis=-1, keepdims=True)
            var = jnp.mean(jnp.square(X - mu), axis=-1, keepdims=True)
            Xn = (X - mu) * jax.lax.rsqrt(var + EPS) * ln_g + ln_b

            def split_heads(t):
                return t.reshape(t.shape[:-1] + (N_HEADS, D_HEAD)).swapaxes(-2, -3)
            Q = split_heads(Xn @ Wq + bq)
            K = split_heads(Xn @ Wk + bk)
            V = split_heads(Xn @ Wv + bv)
            scores = jnp.einsum('bhqd,bhkd->bhqk', Q, K) / jnp.sqrt(jnp.float32(D_HEAD))
            causal = jnp.tril(jnp.ones((n_ctx, n_ctx), dtype=bool))
            scores = jnp.where(causal, scores, jnp.float32(-jnp.inf))
            A = jax.nn.softmax(scores, axis=-1)
            AV = jnp.einsum('bhqk,bhkd->bhqd', A, V)
            AV = AV.swapaxes(-2, -3).reshape(X.shape[:-1] + (D_MODEL,))
            return AV @ Wo + bo
        return _mhsa(X, ln_g, ln_b, Wq, bq, Wk, bk, Wv, bv, Wo, bo)

    def _L0_ffn_ref(input, SU_ug, SU_dp, Wscale_ug, Wscale_dp, W_up, W_gate, W_down):
        import jax, jax.numpy as jnp
        import numpy as np
        HIDDEN = 256
        INTER = 1024
        SCALE = 64.0

        def fwht(x):
            orig_shape = x.shape
            n = orig_shape[-1]
            x = x.reshape(-1, n)
            h = 1
            while h < n:
                x = x.reshape(-1, n // (2 * h), 2, h)
                a, b = (x[:, :, 0, :], x[:, :, 1, :])
                x = jnp.stack([a + b, a - b], axis=2).reshape(-1, n)
                h *= 2
            return (x / jnp.sqrt(jnp.asarray(n, x.dtype))).reshape(orig_shape)
        n = SU_ug.shape[0]
        x = input.reshape(-1, n)
        x = fwht(x * SU_ug) / SCALE
        x_up = x @ W_up.T * (Wscale_ug[:INTER] * SCALE)
        x_gate = x @ W_gate.T * (Wscale_ug[INTER:] * SCALE)
        x = jax.nn.silu(x_gate) * x_up
        x = fwht(x * SU_dp) / SCALE
        x = x @ W_down.T * (Wscale_dp * SCALE)
        return x.reshape(input.shape)
    x = L0_attn_X
    x = x + _L0_attn_ref(_layernorm(x, axis=-1), L0_attn_ln_g, L0_attn_ln_b, L0_attn_Wq, L0_attn_bq, L0_attn_Wk, L0_attn_bk, L0_attn_Wv, L0_attn_bv, L0_attn_Wo, L0_attn_bo)
    x = x + _L0_ffn_ref(_layernorm(x, axis=-1), L0_ffn_SU_ug, L0_ffn_SU_dp, L0_ffn_Wscale_ug, L0_ffn_Wscale_dp, L0_ffn_W_up, L0_ffn_W_gate, L0_ffn_W_down)
    return x

_drawn_inputs = setup_inputs


def setup_inputs(seed=0):
    import zlib

    import numpy as np

    out = dict(_drawn_inputs(seed))
    spreads = {'L0_attn_ln_g': (1.0, 0.6), 'L0_attn_ln_b': (0.0, 0.1)}
    factors = {'L0_attn_Wq': 4.907,
     'L0_attn_bq': 8.0,
     'L0_attn_Wk': 4.881,
     'L0_attn_bk': 8.0,
     'L0_ffn_Wscale_ug': 3.966,
     'L0_ffn_Wscale_dp': 5.517}
    for name, (base, spread) in spreads.items():
        noise = np.random.default_rng([zlib.crc32(name.encode()), seed]).standard_normal(out[name].shape)
        drawn = base * np.exp(spread * noise) if base else spread * noise
        out[name] = jnp.asarray(drawn.astype(out[name].dtype))
    for name, factor in factors.items():
        out[name] = (out[name] * factor).astype(out[name].dtype)
    return out
```

```python
import concourse.bass as bass
from concourse import mybir
from contextlib import ExitStack

SEQ, D, HEADS, INTER = 2048, 256, 16, 1024
P = 128
DH = D // HEADS
TILES = SEQ // P
BW = 512
BLOCKS = SEQ // BW
TPB = BW // P
DC = D // P
IC = INTER // P
HG = 4
GROUPS = HEADS // HG
EPS = 1e-5
START = 1
NEG = -1.0e30
LOWEST = -3.0e38
Q_SLOTS = (0, 0, 0, 1, 1, 2)
K_SLOTS = (0, 1, 2, 0, 1, 0)
ROWS = len(Q_SLOTS) * DH
MROWS = 3
NSLOT = 2 + BLOCKS - 1
PRING = 4
AVLAG = 2
C_G, C_B, C_BQ, C_BK, C_SUG, C_SDP, C_WUG, C_WDP = 0, 2, 4, 6, 8, 10, 18, 34
NCOLS = 36

LEAD = 10
MAX_TILES = ([10], [11, 12, 13], [14, 15], list(range(LEAD)))


def max_jobs(i):
    full, rem = divmod(i, TPB)
    jobs = [("diag", (0, 1, 2, 3), i * P, P, 0)]
    per = BW // (rem * P) if rem else 0
    for h in range(0, HG, per) if rem else ():
        jobs.append(("part", tuple(range(h, h + per)), full * BW, rem * P, 1))
    for f in range(full):
        for h in range(HG):
            jobs.append(("part", (h,), f * BW, BW, 2 + f))
    return jobs


def tile_steps(i):
    steps = [("max", i, k) for k in range(len(max_jobs(i)))]
    if i % TPB == TPB - 1:
        steps.append(("rowmax", i // TPB))
    return steps


def group_steps(last):
    steps, waiting = [], []
    pend_T, pend_norm = None, None
    for b in range(BLOCKS):
        work = []
        for i in MAX_TILES[b]:
            if i < LEAD and last:
                continue
            more = tile_steps(i)
            if pend_T is not None:
                more.insert(len(more) // 2, ("rowmaxT", pend_T))
                pend_T = None
            if i % TPB == TPB - 1:
                pend_T = i // TPB
            work += more
        units = TPB * (b + 1)
        tail = 0
        if b == BLOCKS - 1 and not last:
            tail = len(tile_steps(LEAD - 1)) + len(tile_steps(LEAD - 2))
        body = len(work) - tail
        at = 0
        for j in range(units):
            steps.append(("exp", b, j))
            upto = body * (j + 1) // units
            steps += work[at:upto]
            at = upto
            waiting.append(("av", b, j))
            if len(waiting) > AVLAG:
                steps.append(waiting.pop(0))
                if steps[-1][2] == TPB * (steps[-1][1] + 1) - 1:
                    pend_norm = steps[-1][1]
                    steps.append(("avout", pend_norm))
                elif pend_norm is not None:
                    steps.append(("norm", pend_norm))
                    pend_norm = None
        if pend_T is not None and b != BLOCKS - 1:
            work.append(("rowmaxT", pend_T))
            pend_T = None
        if b < BLOCKS - 1:
            steps += work[at:]
        else:
            n8 = len(tile_steps(LEAD - 2)) if tail else 0
            steps += work[at:at + n8]
            steps += waiting
            steps.append(("avout", b))
            steps += work[at + n8:]
            steps.append(("norm", b))
    return steps


def first_steps():
    steps, pend = [], None
    for i in range(LEAD):
        steps += tile_steps(i)
        if pend is not None:
            steps.append(("rowmaxT", pend))
            pend = None
        if i % TPB == TPB - 1:
            pend = i // TPB
    return steps


FIRST = first_steps()
FIRST_MAX = sum(s[0] == "max" for s in FIRST)
FIRST_RM = sum(s[0] == "rowmax" for s in FIRST)
GROUP_MAX = sum(len(max_jobs(i)) for i in range(TILES))
GROUP_UNITS = sum(TPB * (b + 1) for b in range(BLOCKS))
assert GROUP_MAX % 2 == 0 and GROUP_UNITS % PRING == 0


def unit_no(b, j):
    return sum(TPB * (x + 1) for x in range(b)) + j


def diag_no(b, j):
    return TPB * b + (j - TPB * b) + 1


def build(nc, X, ln_g, ln_b, Wq, bq, Wk, bk, Wv, bv, Wo, bo, SU_ug, SU_dp, Ws_ug, Ws_dp,
          W_up, W_gate, W_down, had, out):
    f32, bf16, f32r = mybir.dt.float32, mybir.dt.bfloat16, mybir.dt.float32r
    ALU = mybir.AluOpType
    ACT = mybir.ActivationFunctionType
    AX = mybir.AxisListType
    ds = bass.ds

    nc.disable_value_cache = True
    ctx = ExitStack()
    with ctx:
        sem_of = {}

        def sem(name):
            sem_of[name] = ctx.enter_context(nc.semaphore(name))
            return sem_of[name]

        size = {f32: 4, f32r: 4, bf16: 2}
        top = [(nc.sbuf_base + 63) // 64 * 64]

        def area(nbytes):
            at = top[0]
            top[0] += (nbytes + 63) // 64 * 64
            return at

        def put(name, shape, dt, at=None):
            n = size[dt]
            for s in shape[1:]:
                n *= s
            if at is None:
                at = area(n)
            return nc.alloc_sbuf_tensor_at(name, shape, dt, offset=at), at + n

        def sb(name, shape, dt):
            return put(name, shape, dt)[0]

        identf = sb("identf", [P, P], f32)
        identb = sb("identb", [P, P], bf16)
        mask = sb("mask", [P, HG, P], bf16)
        hadp = sb("hadp", [P, P], f32)
        hadm = sb("hadm", [P, P], f32)
        rows = sb("rows", [NCOLS, P], f32)
        cols = sb("cols", [P, NCOLS], f32)
        bv_all = sb("bv_all", [P, D], f32)
        bo_all = sb("bo_all", [P, D], f32)
        stats = sb("stats", [P, TILES, 6], f32)
        meanvar = sb("meanvar", [P, TILES, 2], f32)
        halves = sb("halves", [P, TILES], f32)
        var_eps = sb("var_eps", [P, 2, TILES], f32)
        rstd = sb("rstd", [P, 2, TILES], f32)
        lnscale = sb("lnscale", [P, TILES], f32)
        lnshift = sb("lnshift", [P, TILES], f32)
        lntmp = sb("lntmp", [P, TILES], f32)
        pmax = sb("pmax", [P, 2, TPB, HG, NSLOT], f32)
        negmax = sb("negmax", [P, 2, TPB * HG], f32)
        mrest = sb("mrest", [P, 2, TPB * HG], f32)
        mparts = sb("mparts", [P, 2, HG, MROWS, TPB], bf16)
        mrows = sb("mrows", [MROWS * HG * TPB, 2, P], bf16)
        recip = sb("recip", [P, 2, TPB * HG], f32)

        a_ops = area(2 * 2 * HG * SEQ * 2)
        QA, _ = put("QA", [P, 2, HG, SEQ], bf16, a_ops)
        KA, _ = put("KA", [P, 2, HG, SEQ], bf16, a_ops + 2 * HG * SEQ * 2)
        a_v = area(TILES * D * 4)
        V, _ = put("V", [P, TILES, D], f32, a_v)
        a_vg = area(TILES * HG * 32 * 4)
        VG, _ = put("VG", [P, TILES, HG, 32], f32, a_vg)
        a_pr = area(PRING * HG * BW * 4)
        PR, _ = put("PR", [P, PRING, HG, BW], f32, a_pr)
        avT = sb("avT", [P, 2, BW], f32)
        a_o = area(TILES * D * 4)
        xin, _ = put("xin", [P, TILES, D], f32, a_o)
        O, _ = put("O", [P, TILES, D], f32, a_o)
        WUG = sb("WUG", [P, 2 * IC * D], f32)
        WD = sb("WD", [P, IC * D], f32)
        a_e = area(32 * 1024)
        assert top[0] <= nc.sbuf_usable_end, (top[0], nc.sbuf_usable_end)

        XTh, n = put("XTh", [P, 2, DC, BW], f32r, a_e)
        XTl, n = put("XTl", [P, 2, DC, BW], f32r, n)
        xnf, n = put("xnf", [P, 2, BW], f32, n)
        WAh, n = put("WAh", [P, 3, DC, D], f32r, n)
        WAl, n = put("WAl", [P, 3, DC, D], f32r, n)
        wa_raw, _ = put("wa_raw", [P, 3, DC, D], f32, a_vg)
        parts, n = put("parts", [P, 3, 3, BW], bf16, a_pr)
        part_rest, n = put("part_rest", [P, 2, BW], f32, n)
        WT, _ = put("WT", [P, DC, 2 * INTER], f32, a_pr)
        WDx, _ = put("WDx", [P, DC, INTER], f32, a_pr + 16384)
        WDT, _ = put("WDT", [P, IC, D], f32, a_pr)
        wug_raw = WUG[:, :].rearrange("p (t f) -> p t f", f=D)
        wug = WUG[:, :].rearrange("p (c o) -> p c o", c=DC)
        wd_raw = WD[:, :].rearrange("p (c i) -> p c i", c=DC)
        wd = WD[:, :].rearrange("p (c o) -> p c o", c=IC)

        X1, n = put("X1", [P, TILES, D], f32, a_ops)
        X2h, n = put("X2h", [P, DC, SEQ], f32r, n)
        X2l, n = put("X2l", [P, DC, SEQ], f32r, n)
        Hh, n = put("Hh", [P, 4, BW], f32r, n)
        Hl, n = put("Hl", [P, 4, BW], f32r, n)
        UGh, n = put("UGh", [P, DC, 2 * INTER], f32r, a_pr)
        UGl, n = put("UGl", [P, DC, 2 * INTER], f32r, n)
        Dh, n = put("Dh", [P, IC, D], f32r, a_v)
        Dl, n = put("Dl", [P, IC, D], f32r, n)
        OTh, n = put("OTh", [P, DC, BW], f32r, a_vg)
        OTl, n = put("OTl", [P, DC, BW], f32r, n)
        wo_raw, n = put("wo_raw", [P, DC, D], f32, a_e)
        Woh, n = put("Woh", [P, DC, D], f32r, n)
        Wol, n = put("Wol", [P, DC, D], f32r, n)
        sg, n = put("sg", [P, 2, BW], f32, n)
        hf, n = put("hf", [P, 2, BW], f32, n)
        yst, n = put("yst", [P, TPB, D], f32, n)
        xh2, n = put("xh2", [P, 2, TPB, D], f32, n)
        assert n <= a_e + 32 * 1024

        psS = ctx.enter_context(nc.psum_tensor("psS", [P, 2, BW], f32))
        psT = ctx.enter_context(nc.psum_tensor("psT", [P, 4, BW], f32))
        psA = ctx.enter_context(nc.psum_tensor("psA", [P, BW], f32))
        psM = ctx.enter_context(nc.psum_tensor("psM", [P, BW], f32))
        psMb = psM[:, :].bitcast(bf16)

        scr = nc.dram_tensor("scr", (2, 3, D, SEQ), bf16, kind="Internal").ap()

        x_in = [sem(f"x_in{b}") for b in range(BLOCKS)]
        rows_in, wa_in, bias_in, had_in, wffn_in = (sem(n) for n in
            ("rows_in", "wa_in", "bias_in", "had_in", "wffn_in"))
        dve_link, pool_link = sem("dve_link"), sem("pool_link")
        consts_ready, halves_ready = sem("consts_ready"), sem("halves_ready")
        hadm_ready = sem("hadm_ready")
        pool_waited, pe_waited = sem("pool_waited"), sem("pe_waited")
        rowsT, cols_ready = sem("rowsT"), sem("cols_ready")
        var_ready, rstd_ready, xh_ready = sem("var_ready"), sem("rstd_ready"), sem("xh_ready")
        xT, xnf_ready, xsplit = sem("xT"), sem("xnf_ready"), sem("xsplit")
        wa_split = sem("wa_split")
        qk_proj, part0, rest_ready, parts_ready = (sem(n) for n in
            ("qk_proj", "part0", "rest_ready", "parts_ready"))
        scr_out = [sem(f"scr_out{i}") for i in range(3)]
        v_proj, v_ready = sem("v_proj"), sem("v_ready")
        ops_in = sem("ops_in")
        wd_rot, prep_mm, prep_evac = sem("wd_rot"), sem("prep_mm"), sem("prep_evac")
        vg_ready = sem("vg_ready")
        max_scores, max_done = sem("max_scores"), sem("max_done")
        rowmax_ready, mparts_ready, mrowsT, mrows_ready = (sem(n) for n in
            ("rowmax_ready", "mparts_ready", "mrowsT", "mrows_ready"))
        mrows_in = [sem(f"mrows_in{i}") for i in range(2)]
        scores, probs, masked, av_done, av_out = (sem(n) for n in
            ("scores", "probs", "masked", "av_done", "av_out"))
        avT_done, recip_ready, norm_done = sem("avT_done"), sem("recip_ready"), sem("norm_done")
        xre_in, wo_in, xb_ready, wsplit_hi, wsplit = (sem(n) for n in
            ("xre_in", "wo_in", "xb_ready", "wsplit_hi", "wsplit"))
        oT, oT_hi, oT_split, o_proj, x1_ready = (sem(n) for n in
            ("oT", "oT_hi", "oT_split", "o_proj", "x1_ready"))
        var2, rstd2, xh2_ready, x2T, x2_hi, x2_split = (sem(n) for n in
            ("var2", "rstd2", "xh2_ready", "x2T", "x2_hi", "x2_split"))
        ug_mm, silu_ready, h_ready, h_hi, h_split, down_k, y_ready, y_out = (sem(n) for n in
            ("ug_mm", "silu_ready", "h_ready", "h_hi", "h_split", "down_k", "y_ready", "y_out"))

        block = ctx.enter_context(nc.Block())

        def at(t, par, *rest):
            v = t[rest[0], ds(par, 1), rest[1], rest[2]]
            return v.rearrange("p a n -> p (a n)")

        QK_ROUNDS = [(b, w, half) for b in range(BLOCKS) for w in range(2) for half in range(DC)]

        def down_bank(t):
            return (psS[:, 0, 0:D], psS[:, 1, 0:D], psA[:, 0:D], psM[:, 0:D])[t]

        @block.sync
        def _(sp):
            sp.sem_inc(y_out, START)
            x_t = X.rearrange("a (t p) f -> p (a t) f", p=P)
            for b in range(BLOCKS):
                sp.dma_start(xin[:, b * TPB:(b + 1) * TPB, :],
                             x_t[:, b * TPB:(b + 1) * TPB, :]).then_inc(x_in[b], 16)
                if b == 0:
                    for c, v in ((C_G, ln_g), (C_B, ln_b), (C_BQ, bq), (C_BK, bk), (C_SUG, SU_ug),
                                 (C_SDP, SU_dp), (C_WUG, Ws_ug), (C_WDP, Ws_dp)):
                        v = v.rearrange("(c p) -> c p", p=P)
                        sp.dma_start(rows[c:c + v.shape[0], :], v).then_inc(rows_in, 16)
            for w, src in enumerate((Wq, Wk, Wv)):
                sp.dma_start(wa_raw[:, w, :, :], src.rearrange("(c p) n -> p c n", p=P)).then_inc(wa_in, 16)
            for dst, src in ((bv_all, bv), (bo_all, bo)):
                sp.dma_start(dst[:, :], src.rearrange("(a n) -> a n", a=1).to_broadcast([P, D]))\
                  .then_inc(bias_in, 16)
            sp.dma_start(hadp[:, :], had).then_inc(had_in, 16)
            for n, src in enumerate((W_up, W_gate)):
                sp.dma_start(wug_raw[:, n * IC:(n + 1) * IC, :],
                             src.rearrange("(t o) f -> o t f", o=P)).then_inc(wffn_in, 16)
            sp.dma_start(wd_raw, W_down.rearrange("(c o) i -> o c i", o=P)).then_inc(wffn_in, 16)

            for r, (b, w, half) in enumerate(QK_ROUNDS):
                sp.wait_ge(parts_ready, r + 1)
                sp.dma_start(scr[w, :, half * P:(half + 1) * P, b * BW:(b + 1) * BW]
                             .rearrange("s f n -> f s n"), parts[:, r % 3, :, :]).then_inc(scr_out[r % 3], 16)
            for i in range(3):
                sp.wait_ge(scr_out[i], 16 * len(QK_ROUNDS[i::3]))

            def load_group(g):
                for w, (dst, slots) in enumerate(((QA, Q_SLOTS), (KA, K_SLOTS))):
                    for s, part in enumerate(slots):
                        src = scr[w, part, ds(g * (HG * DH), HG * DH), :].rearrange("(h d) n -> d h n", d=DH)
                        sp.dma_start(dst[s * DH:(s + 1) * DH, ds(g % 2, 1), :, :]
                                     .rearrange("d a h n -> d (a h) n"), src).then_inc(ops_in, 16)

            def store_max(g, b, n):
                sp.wait_ge(mrows_ready, n + 1)
                for h in range(HG):
                    dst = QA[ROWS:ROWS + MROWS, ds(g % 2, 1), h, b * BW:(b + 1) * BW]\
                        .rearrange("m a (t q) -> m (a t) q", t=TPB)
                    sp.dma_start(dst, mrows[h * MROWS * TPB:(h + 1) * MROWS * TPB, b % 2, :])\
                      .then_inc(mrows_in[b % 2], 16)

            load_group(0)
            for s in FIRST:
                if s[0] == "rowmaxT":
                    store_max(0, s[1], s[1])

            def group(g, last):
                if not last:
                    sp.wait_ge(av_done, g * GROUP_UNITS + START)
                    sp.wait_ge(ops_in, (g + 1) * (16 * 12))
                    load_group(g + 1)
                n = 0
                for s in group_steps(last):
                    if s[0] == "rowmaxT":
                        nxt = s[1] * TPB + TPB - 1 < LEAD
                        store_max(g + 1 if nxt else g, s[1], g * BLOCKS + FIRST_RM + n)
                        n += 1

            with sp.Fori(0, GROUPS - 1) as g:
                group(g, False)
            group(GROUPS - 1, True)

            sp.wait_ge(av_done, GROUPS * GROUP_UNITS + START)
            sp.dma_start(X1[:, :, :], x_t).then_inc(xre_in, 16)
            sp.dma_start(wo_raw[:, :, :], Wo.rearrange("(c p) n -> p c n", p=P)).then_inc(wo_in, 16)
            out_t = out.rearrange("a (t p) f -> p (a t) f", p=P)
            with sp.Fori(0, BLOCKS) as b:
                sp.wait_ge(y_ready, b * TPB + TPB + START)
                sp.dma_start(out_t[:, ds(b * TPB, TPB), :], yst[:, :, :]).then_inc(y_out, 16)
            sp.wait_ge(y_out, 16 * BLOCKS + START)

        @block.gpsimd
        def _(pool):
            chain = [0]

            def link(ins):
                chain[0] += 1
                ins.then_inc(pool_link, 1)
                pool.wait_ge(pool_link, chain[0])

            nc.gpsimd.memset(halves[:, :], -0.5).then_inc(halves_ready, 1)
            nc.gpsimd.memset(identf[:, :], 0.0)
            nc.gpsimd.memset(identb[:, :], 0.0)
            link(nc.gpsimd.memset(mask[:, :, :], 0.0))
            nc.gpsimd.affine_select(out=identf[:, :], in_=identf[:, :], compare_op=ALU.not_equal, fill=1.0,
                                    base=0, pattern=[[-1, P]], channel_multiplier=1).then_inc(consts_ready, 1)
            nc.gpsimd.affine_select(out=identb[:, :], in_=identb[:, :], compare_op=ALU.not_equal, fill=1.0,
                                    base=0, pattern=[[-1, P]], channel_multiplier=1).then_inc(consts_ready, 1)
            nc.gpsimd.affine_select(out=mask[:, :, :], in_=mask[:, :, :], compare_op=ALU.is_ge, fill=NEG,
                                    base=0, pattern=[[0, HG], [-1, P]], channel_multiplier=1)\
                .then_inc(consts_ready, 1)
            nc.gpsimd.memset(pmax[:, :, :, :, :], LOWEST).then_inc(consts_ready, 1)

            def power(n):
                pool.wait_ge(var_ready, n + 1)
                nc.gpsimd.tensor_tensor(out=rstd[:, n, :], in0=var_eps[:, n, :], in1=halves[:, :],
                                        op=ALU.pow).then_inc(rstd_ready, 1)

            pool.wait_ge(wa_in, 48)
            link(nc.gpsimd.tensor_copy(WAh[:, :, :, :], wa_raw[:, :, :, :]))
            link(nc.gpsimd.tensor_tensor(out=WAl[:, :, :, :], in0=wa_raw[:, :, :, :],
                                         in1=WAh[:, :, :, :].bitcast(f32), op=ALU.subtract))
            nc.gpsimd.memset(VG[:, :, :, :], 1.0).then_inc(wa_split, 1)
            power(0)
            power(1)
            pool.wait_ge(rstd_ready, 2)
            nc.gpsimd.memset(KA[ROWS:ROWS + MROWS, :, :, :], 1.0).then_inc(consts_ready, 1)
            pool.wait_ge(consts_ready, 5)
            pool.wait_ge(had_in, 16)
            nc.gpsimd.tensor_scalar(hadm[:, :], hadp[:, :], -1.0, None, ALU.mult).then_inc(hadm_ready, 1)

            for r in range(len(QK_ROUNDS)):
                pool.wait_ge(rest_ready, r + 1)
                link(nc.gpsimd.tensor_copy(parts[:, r % 3, 1, :], part_rest[:, r % 2, :]))
                nc.gpsimd.tensor_tensor(out=parts[:, r % 3, 2, :], in0=part_rest[:, r % 2, :],
                                        in1=parts[:, r % 3, 1, :], op=ALU.subtract).then_inc(parts_ready, 1)

            pool.wait_ge(wffn_in, 48)
            pool.wait_ge(cols_ready, 1)
            for c in range(DC):
                link(nc.gpsimd.tensor_scalar(wd_raw[:, c, :], wd_raw[:, c, :], cols[:, C_WDP + c:C_WDP + c + 1],
                                             float(INTER) ** -0.5, ALU.mult, ALU.mult))
            src, dst = wd_raw, WDx[:, :, :]
            for step in range(3):
                w = P << step
                a = src.rearrange("p c (m two w) -> p (c m) two w", two=2, w=w)
                o = dst.rearrange("p c (m two w) -> p (c m) two w", two=2, w=w)
                link(nc.gpsimd.tensor_tensor(out=o[:, :, 0, :], in0=a[:, :, 0, :], in1=a[:, :, 1, :], op=ALU.add))
                last = nc.gpsimd.tensor_tensor(out=o[:, :, 1, :], in0=a[:, :, 0, :], in1=a[:, :, 1, :],
                                               op=ALU.subtract)
                if step < 2:
                    link(last)
                    src, dst = dst, src
            last.then_inc(wd_rot, 1)

            def load_vg(g, c):
                src = V[:, c * TPB:(c + 1) * TPB, ds(g * (HG * DH), HG * DH)]\
                    .rearrange("p t (h d) -> p t h d", d=DH)
                nc.gpsimd.tensor_copy(VG[:, c * TPB:(c + 1) * TPB, :, 0:DH], src).then_inc(vg_ready, 1)

            pool.wait_ge(v_ready, TILES // 2)
            pool.wait_ge(v_proj, TILES // 2)
            for c in range(BLOCKS):
                load_vg(0, c)

            def split_max(b, n):
                pool.wait_ge(rowmax_ready, n + 1)
                if not (isinstance(n, int) and n < 2):
                    pool.wait_ge(mrowsT, n - 1)
                pool.sem_inc(pool_waited, 1)
                k = b % 2
                part = [mparts[:, k, :, m, :] for m in range(MROWS)]
                whole, rest = (x[:, k, :].rearrange("p (h t) -> p h t", h=HG) for x in (negmax, mrest))
                steps = ((part[0], whole, None), (rest, whole, part[0]),
                         (part[1], rest, None), (part[2], rest, part[1]))
                for i, (o, a, minus) in enumerate(steps):
                    if minus is None:
                        ins = nc.gpsimd.tensor_copy(o, a)
                    else:
                        ins = nc.gpsimd.tensor_tensor(out=o, in0=a, in1=minus, op=ALU.subtract)
                    if i < 3:
                        ins.then_inc(pool_link, 1)
                        pool.wait_ge(pool_link, n * 3 + chain[0] + i + 1)
                        pool.sem_inc(pool_waited, 1)
                    else:
                        ins.then_inc(mparts_ready, 1)

            for s in FIRST:
                if s[0] == "rowmax":
                    split_max(s[1], s[1])

            def group(g, last):
                n = 0
                units = g * GROUP_UNITS
                for s in group_steps(last):
                    if s[0] == "rowmax":
                        split_max(s[1], g * BLOCKS + FIRST_RM + n)
                        n += 1
                    elif s[0] == "exp" and s[2] >= TPB * s[1]:
                        _, b, j = s
                        u = unit_no(b, j)
                        off = (j - TPB * b) * P
                        pool.wait_ge(probs, (units + u) * 2 + 2 + START)
                        pool.sem_inc(pool_waited, 1)
                        v = PR[:, u % PRING, :, off:off + P]
                        nc.gpsimd.affine_select(out=v, in_=v, compare_op=ALU.is_ge, fill=0.0, base=0,
                                                pattern=[[0, HG], [1, P]], channel_multiplier=-1)\
                            .then_inc(masked, 1)
                    elif s[0] == "av" and s[1] == BLOCKS - 1 and s[2] % TPB == TPB - 1 and not last:
                        pool.wait_ge(av_done, units + unit_no(s[1], s[2]) + 1 + START)
                        pool.sem_inc(pool_waited, 1)
                        load_vg(g + 1, s[2] // TPB)

            with pool.Fori(0, GROUPS - 1) as g:
                group(g, False)
            group(GROUPS - 1, True)

            pool.wait_ge(xre_in, 16)
            for b in range(BLOCKS):
                v = X1[:, b * TPB:(b + 1) * TPB, :]
                nc.gpsimd.tensor_tensor(out=v, in0=v, in1=bo_all[:, :].unsqueeze(1).to_broadcast([P, TPB, D]),
                                        op=ALU.add).then_inc(xb_ready, 1)
            for b in range(BLOCKS):
                k = b * TPB
                pool.wait_ge(var2, b + 1)
                nc.gpsimd.tensor_tensor(out=rstd[:, 0, k:k + TPB], in0=var_eps[:, 0, k:k + TPB],
                                        in1=halves[:, k:k + TPB], op=ALU.pow).then_inc(rstd2, 1)

        @block.scalar
        def _(act):
            for s in (probs, av_out, h_hi):
                act.sem_inc(s, START)
            act.wait_ge(cols_ready, 1)

            def norm_x(b):
                for c in range(DC):
                    n = b * DC + c
                    act.wait_ge(xT, n + 1)
                    if n >= 2:
                        act.wait_ge(xsplit, n - 1)
                    nc.scalar.activation(xnf[:, n % 2, :], psS[:, n % 2, :], ACT.Identity,
                                         bias=cols[:, C_B + c:C_B + c + 1],
                                         scale=cols[:, C_G + c:C_G + c + 1]).then_inc(xnf_ready, 1)

            norm_x(0)
            for b in range(BLOCKS):
                if b + 1 < BLOCKS:
                    norm_x(b + 1)
                for r in range(4 * b, 4 * b + 4):
                    _, w, half = QK_ROUNDS[r]
                    c = (C_BQ, C_BK)[w] + half
                    act.wait_ge(qk_proj, r + 1)
                    if r >= 3:
                        act.wait_ge(scr_out[r % 3], 16 * (r // 3))
                    nc.scalar.activation(parts[:, r % 3, 0, :], psT[:, r % 4, :], ACT.Identity,
                                         bias=cols[:, c:c + 1]).then_inc(part0, 1)

            for i in range(3):
                act.wait_ge(scr_out[i], 16 * len(QK_ROUNDS[i::3]))
            n = 0
            for c in range(DC):
                for q in range(4):
                    act.wait_ge(prep_mm, n + 1)
                    nc.scalar.activation(WT[:, c, q * BW:(q + 1) * BW], psT[:, n % 4, :], ACT.Copy,
                                         scale=float(D) ** -0.5).then_inc(prep_evac, 1)
                    n += 1
            for c in range(DC):
                for q in range(4):
                    act.wait_ge(prep_mm, n + 1)
                    nc.scalar.activation(wug[:, c, q * BW:(q + 1) * BW], psT[:, n % 4, :], ACT.Copy,
                                         scale=cols[:, C_SUG + c:C_SUG + c + 1]).then_inc(prep_evac, 1)
                    n += 1
            for q in range(4):
                act.wait_ge(prep_mm, n + 1)
                nc.scalar.activation(WDT[:, 2 * q:2 * q + 2, :].rearrange("p c o -> p (c o)"),
                                     psT[:, n % 4, :], ACT.Copy).then_inc(prep_evac, 1)
                n += 1
            for q in range(4):
                act.wait_ge(prep_mm, n + 1)
                for j in range(2):
                    c = 2 * q + j
                    last = nc.scalar.activation(wd[:, c, :], psT[:, n % 4, j * D:(j + 1) * D], ACT.Copy,
                                                scale=cols[:, C_SDP + c:C_SDP + c + 1])
                last.then_inc(prep_evac, 1)
                n += 1

            def max_rows(b, n, before):
                act.wait_ge(mrowsT, n + 1)
                act.wait_ge(mrows_in[b % 2], before * (16 * HG))
                nc.scalar.activation(mrows[:, b % 2, :], psMb[0:MROWS * HG * TPB, 0:P], ACT.Copy)\
                    .then_inc(mrows_ready, 1)

            for s in FIRST:
                if s[0] == "rowmaxT":
                    max_rows(s[1], s[1], 0)

            def group(g, last):
                units = g * GROUP_UNITS
                n = 0
                for s in group_steps(last):
                    if s[0] == "rowmaxT":
                        max_rows(s[1], g * BLOCKS + FIRST_RM + n, g * (BLOCKS // 2) + (FIRST_RM + n) // 2)
                        n += 1
                    elif s[0] == "exp":
                        _, b, j = s
                        u = unit_no(b, j)
                        off = max(j - TPB * b, 0) * P
                        for pair in range(2):
                            act.wait_ge(scores, (units + u) * 2 + pair + 1)
                            if pair == 0:
                                act.wait_ge(av_done, units + u + first_free(g, u) + START)
                            nc.scalar.activation(PR[:, u % PRING, 2 * pair:2 * pair + 2, off:BW],
                                                 psT[:, 2 * pair:2 * pair + 2, off:BW], ACT.Exp,
                                                 scale=float(DH) ** -0.5).then_inc(probs, 1)
                    elif s[0] == "avout":
                        b = s[1]
                        act.wait_ge(av_done, units + unit_no(b, TPB * (b + 1) - 1) + 1 + START)
                        if b >= 2:
                            act.wait_ge(avT_done, g * BLOCKS + b - 1 + START)
                        else:
                            act.wait_ge(avT_done, g * BLOCKS + START)
                        nc.scalar.activation(avT[:, b % 2, :], psA[:, :], ACT.Copy).then_inc(av_out, 1)

            def first_free(g, u):
                return 1 - PRING if u >= PRING else -u

            with act.Fori(0, GROUPS - 1) as g:
                group(g, False)
            group(GROUPS - 1, True)

            act.wait_ge(av_done, GROUPS * GROUP_UNITS + START)
            act.wait_ge(wo_in, 16)
            nc.scalar.activation(Woh[:, :, :], wo_raw[:, :, :], ACT.Copy).then_inc(wsplit_hi, 1)

            def hi_from_psum(full, done, n, dst, bank):
                act.wait_ge(full, n + 1)
                nc.scalar.activation(dst, bank, ACT.Copy).then_inc(done, 1)

            def split_big(k):
                if k < 2:
                    nc.scalar.activation(UGh[:, k, :], wug[:, k, :], ACT.Copy).then_inc(wsplit_hi, 1)
                else:
                    nc.scalar.activation(Dh[:, :, :], wd, ACT.Copy).then_inc(wsplit_hi, 1)

            def attn_out(b):
                for c in range(DC):
                    n = b * DC + c
                    act.wait_ge(oT, n + 1)
                    if b >= 1:
                        act.wait_ge(o_proj, 2 * b)
                    nc.scalar.activation(OTh[:, c, :], psS[:, c, :], ACT.Copy).then_inc(oT_hi, 1)

            def norm2(b):
                for c in range(DC):
                    n = b * DC + c
                    act.wait_ge(x2T, n + 1)
                    nc.scalar.activation(X2h[:, c, b * BW:(b + 1) * BW], psT[:, 2 + c, :], ACT.Copy)\
                        .then_inc(x2_hi, 1)

            for b in range(BLOCKS):
                attn_out(b)
                if b < 3:
                    split_big(b)
                if b >= 1:
                    norm2(b - 1)
            norm2(BLOCKS - 1)

            with act.Fori(0, BLOCKS) as b:
                for k in range(IC):
                    act.wait_ge(ug_mm, b * IC + k + 1)
                    if k >= 2:
                        act.wait_ge(h_ready, b * IC + k - 1 + START)
                    else:
                        act.wait_ge(h_ready, b * IC + START)
                    nc.scalar.activation(sg[:, k % 2, :], psT[:, 2 * (k % 2), :], ACT.Silu,
                                         scale=cols[:, C_WUG + IC + k:C_WUG + IC + k + 1])\
                        .then_inc(silu_ready, 1)
                    act.wait_ge(h_ready, b * IC + k + 1 + START)
                    if k >= 4:
                        act.wait_ge(down_k, b * IC + k - 3 + START)
                    else:
                        act.wait_ge(down_k, b * IC + START)
                    nc.scalar.activation(Hh[:, k % 4, :], hf[:, k % 2, :], ACT.Copy).then_inc(h_hi, 1)

        @block.vector
        def _(dve):
            for s in (norm_done, h_ready, y_ready):
                dve.sem_inc(s, START)
            chain = [0]

            def link(ins):
                chain[0] += 1
                ins.then_inc(dve_link, 1)
                dve.wait_ge(dve_link, chain[0])

            for b in range(BLOCKS):
                dve.wait_ge(x_in[b], 16)
                for t in range(b * TPB, (b + 1) * TPB):
                    last = nc.vector.bn_stats(stats[:, t, :], xin[:, t, :])
            link(last)
            for t in range(TILES):
                last = nc.vector.bn_aggr(meanvar[:, t, :], stats[:, t, :])
            link(last)
            mean, var = meanvar[:, :, 0], meanvar[:, :, 1]
            nc.vector.tensor_scalar(var_eps[:, 0, :], var, EPS, None, ALU.add).then_inc(var_ready, 1)
            dve.wait_ge(rowsT, 1)
            nc.vector.tensor_copy(cols[:, :], psM[:, 0:NCOLS]).then_inc(cols_ready, 1)
            dve.wait_ge(rstd_ready, 1)
            link(nc.vector.tensor_tensor(out=lntmp[:, :], in0=var, in1=rstd[:, 0, :], op=ALU.mult))
            link(nc.vector.tensor_tensor(out=lntmp[:, :], in0=lntmp[:, :], in1=rstd[:, 0, :], op=ALU.mult))
            nc.vector.tensor_scalar(var_eps[:, 1, :], lntmp[:, :], EPS, None, ALU.add).then_inc(var_ready, 1)
            dve.wait_ge(rstd_ready, 2)
            link(nc.vector.tensor_tensor(out=lnscale[:, :], in0=rstd[:, 0, :], in1=rstd[:, 1, :], op=ALU.mult))
            link(nc.vector.scalar_tensor_tensor(out=lnshift[:, :], in0=mean, scalar=-1.0, in1=lnscale[:, :],
                                                op0=ALU.mult, op1=ALU.mult))

            def scale_x(b):
                for t in range(b * TPB, (b + 1) * TPB):
                    nc.vector.tensor_scalar(xin[:, t, :], xin[:, t, :], lnscale[:, t:t + 1],
                                            lnshift[:, t:t + 1], ALU.mult, ALU.add).then_inc(xh_ready, 1)

            def split_x(b):
                for c in range(DC):
                    n = b * DC + c
                    dve.wait_ge(xnf_ready, n + 1)
                    if b >= 2:
                        dve.wait_ge(v_proj, 2 * (b - 1))
                    link(nc.vector.tensor_copy(XTh[:, b % 2, c, :], xnf[:, n % 2, :]))
                    nc.vector.tensor_tensor(out=XTl[:, b % 2, c, :], in0=xnf[:, n % 2, :],
                                            in1=XTh[:, b % 2, c, :].bitcast(f32),
                                            op=ALU.subtract).then_inc(xsplit, 1)

            scale_x(0)
            scale_x(1)
            split_x(0)
            dve.wait_ge(bias_in, 32)
            for b in range(BLOCKS):
                if b + 2 < BLOCKS:
                    scale_x(b + 2)
                if b + 1 < BLOCKS:
                    split_x(b + 1)
                for r in range(4 * b, 4 * b + 4):
                    _, w, half = QK_ROUNDS[r]
                    c = (C_BQ, C_BK)[w] + half
                    dve.wait_ge(part0, r + 1)
                    if r >= 2:
                        dve.wait_ge(parts_ready, r - 1)
                    nc.vector.scalar_tensor_tensor(out=part_rest[:, r % 2, :], in0=psT[:, r % 4, :],
                                                   scalar=cols[:, c:c + 1], in1=parts[:, r % 3, 0, :],
                                                   op0=ALU.add, op1=ALU.subtract).then_inc(rest_ready, 1)
                for v in range(2 * b, 2 * b + 2):
                    dve.wait_ge(v_proj, v + 1)
                    bank = (psA, psM)[v % 2]
                    nc.vector.tensor_tensor(out=V[:, 2 * v:2 * v + 2, :],
                                            in0=bank[:, :].rearrange("p (t n) -> p t n", t=2),
                                            in1=bv_all[:, :].unsqueeze(1).to_broadcast([P, 2, D]),
                                            op=ALU.add).then_inc(v_ready, 1)

            dve.wait_ge(consts_ready, 4)

            def reduce_bank(i, k, n, bank):
                _, heads, _, width, slot = max_jobs(i)[k]
                dve.wait_ge(max_scores, n + 1)
                nc.vector.tensor_reduce(pmax[:, (i // TPB) % 2, i % TPB, heads[0]:heads[-1] + 1, slot],
                                        psS[:, bank, 0:len(heads) * width]
                                        .rearrange("p (h n) -> p h n", n=width),
                                        axis=AX.X, op=ALU.max).then_inc(max_done, 1)

            def block_max(b, banks, n):
                dve.wait_ge(max_done, banks)
                if not (isinstance(n, int) and n < 2):
                    dve.wait_ge(mparts_ready, n - 1)
                nc.vector.tensor_reduce(negmax[:, b % 2, :].rearrange("p (h t) -> p t h", t=TPB),
                                        pmax[:, b % 2, :, :, 0:2 + b],
                                        axis=AX.X, op=ALU.max, negate=True).then_inc(rowmax_ready, 1)

            n = 0
            for s in FIRST:
                if s[0] == "max":
                    reduce_bank(s[1], s[2], n, n % 2)
                    n += 1
                elif s[0] == "rowmax":
                    block_max(s[1], n, s[1])

            def group(g, last):
                n = m = 0
                for s in group_steps(last):
                    if s[0] == "max":
                        reduce_bank(s[1], s[2], g * GROUP_MAX + FIRST_MAX + n, (FIRST_MAX + n) % 2)
                        n += 1
                    elif s[0] == "rowmax":
                        block_max(s[1], g * GROUP_MAX + FIRST_MAX + n, g * BLOCKS + FIRST_RM + m)
                        m += 1
                    elif s[0] == "norm":
                        b = s[1]
                        dve.wait_ge(avT_done, g * BLOCKS + b + 1 + START)
                        v = psM[:, :].rearrange("p (t h n) -> p t h n", t=TPB, h=HG)
                        nc.vector.reciprocal(recip[:, b % 2, :].rearrange("p (t h) -> p t h", t=TPB),
                                             v[:, :, :, DH]).then_inc(recip_ready, 1)
                        dve.wait_ge(recip_ready, g * BLOCKS + b + 1)
                        o = O[:, b * TPB:(b + 1) * TPB, ds(g * (HG * DH), HG * DH)]\
                            .rearrange("p t (h d) -> p t h d", d=DH)
                        r = recip[:, b % 2, :].rearrange("p (t h) -> p t h", t=TPB)\
                            .unsqueeze(3).to_broadcast([P, TPB, HG, DH])
                        nc.vector.tensor_tensor(out=o, in0=v[:, :, :, 0:DH], in1=r,
                                                op=ALU.mult).then_inc(norm_done, 1)

            with dve.Fori(0, GROUPS - 1) as g:
                group(g, False)
            group(GROUPS - 1, True)

            dve.wait_ge(wsplit_hi, 1)
            nc.vector.tensor_tensor(out=Wol[:, :, :], in0=wo_raw[:, :, :], in1=Woh[:, :, :].bitcast(f32),
                                    op=ALU.subtract).then_inc(wsplit, 1)

            def split_big(k):
                dve.wait_ge(wsplit_hi, k + 2)
                if k < 2:
                    nc.vector.tensor_tensor(out=UGl[:, k, :], in0=wug[:, k, :], in1=UGh[:, k, :].bitcast(f32),
                                            op=ALU.subtract).then_inc(wsplit, 1)
                else:
                    nc.vector.tensor_tensor(out=Dl[:, :, :], in0=wd, in1=Dh[:, :, :].bitcast(f32),
                                            op=ALU.subtract).then_inc(wsplit, 1)

            def attn_out(b):
                for c in range(DC):
                    dve.wait_ge(oT_hi, b * DC + c + 1)
                    nc.vector.tensor_tensor(out=OTl[:, c, :], in0=psS[:, c, :], in1=OTh[:, c, :].bitcast(f32),
                                            op=ALU.subtract).then_inc(oT_split, 1)

            def residual(b):
                dve.wait_ge(xb_ready, b + 1)
                for v in range(2):
                    dve.wait_ge(o_proj, 2 * b + v + 1)
                    t = b * TPB + 2 * v
                    ins = nc.vector.tensor_tensor(out=X1[:, t:t + 2, :],
                                                  in0=psT[:, v, :].rearrange("p (t n) -> p t n", t=2),
                                                  in1=X1[:, t:t + 2, :], op=ALU.add)
                    ins.then_inc(x1_ready, 1)
                dve.wait_ge(x1_ready, 2 * b + 2)
                ts = range(b * TPB, (b + 1) * TPB)
                for t in ts:
                    last = nc.vector.bn_stats(stats[:, t, :], X1[:, t, :])
                link(last)
                for t in ts:
                    last = nc.vector.bn_aggr(meanvar[:, t, :], stats[:, t, :])
                link(last)
                k = b * TPB
                nc.vector.tensor_scalar(var_eps[:, 0, k:k + TPB], meanvar[:, k:k + TPB, 1], EPS, None,
                                        ALU.add).then_inc(var2, 1)

            def norm2(b):
                k = b * TPB
                dve.wait_ge(rstd2, b + 1)
                link(nc.vector.scalar_tensor_tensor(out=lnshift[:, k:k + TPB], in0=meanvar[:, k:k + TPB, 0],
                                                    scalar=-1.0, in1=rstd[:, 0, k:k + TPB],
                                                    op0=ALU.mult, op1=ALU.mult))
                if b >= 2:
                    dve.wait_ge(x2T, DC * (b - 1))
                for t in range(TPB):
                    last = nc.vector.tensor_scalar(xh2[:, b % 2, t, :], X1[:, k + t, :],
                                                   rstd[:, 0, k + t:k + t + 1], lnshift[:, k + t:k + t + 1],
                                                   ALU.mult, ALU.add)
                last.then_inc(xh2_ready, 1)

            def split_x2(b):
                for c in range(DC):
                    dve.wait_ge(x2_hi, b * DC + c + 1)
                    v = slice(b * BW, (b + 1) * BW)
                    nc.vector.tensor_tensor(out=X2l[:, c, v], in0=psT[:, 2 + c, :],
                                            in1=X2h[:, c, v].bitcast(f32),
                                            op=ALU.subtract).then_inc(x2_split, 1)

            for b in range(BLOCKS):
                attn_out(b)
                residual(b)
                if b < 3:
                    split_big(b)
                norm2(b)
                if b >= 1:
                    split_x2(b - 1)
            split_x2(BLOCKS - 1)

            with dve.Fori(0, BLOCKS) as b:
                for k in range(IC):
                    dve.wait_ge(silu_ready, b * IC + k + 1)
                    if k >= 2:
                        dve.wait_ge(h_hi, b * IC + k - 1 + START)
                    else:
                        dve.wait_ge(h_hi, b * IC + START)
                    nc.vector.scalar_tensor_tensor(out=hf[:, k % 2, :], in0=psT[:, 2 * (k % 2) + 1, :],
                                                   scalar=cols[:, C_WUG + k:C_WUG + k + 1],
                                                   in1=sg[:, k % 2, :], op0=ALU.mult,
                                                   op1=ALU.mult).then_inc(h_ready, 1)
                    dve.wait_ge(h_hi, b * IC + k + 1 + START)
                    nc.vector.tensor_tensor(out=Hl[:, k % 4, :], in0=hf[:, k % 2, :],
                                            in1=Hh[:, k % 4, :].bitcast(f32),
                                            op=ALU.subtract).then_inc(h_split, 1)
                dve.wait_ge(y_out, b * 16 + START)
                dve.wait_ge(down_k, b * IC + IC + START)
                for t in range(TPB):
                    nc.vector.tensor_tensor(out=yst[:, t, :], in0=down_bank(t),
                                            in1=X1[:, ds(b * TPB + t, 1), :].rearrange("p a n -> p (a n)"),
                                            op=ALU.add).then_inc(y_ready, 1)

        @block.tensor
        def _(pe):
            for s in (av_done, avT_done, down_k):
                pe.sem_inc(s, START)
            pe.wait_ge(consts_ready, 2)
            pe.wait_ge(rows_in, 16 * 8)
            nc.tensor.transpose(psM[:, 0:NCOLS], rows[:, :], identf[0:NCOLS, 0:NCOLS]).then_inc(rowsT, 1)

            def transpose_x(b):
                pe.wait_ge(xh_ready, TPB * (b + 1))
                for c in range(DC):
                    n = b * DC + c
                    if n >= 2:
                        pe.wait_ge(xnf_ready, n - 1)
                    for t in range(TPB):
                        last = nc.tensor.transpose(psS[:, n % 2, t * P:(t + 1) * P],
                                                   xin[:, b * TPB + t, c * P:(c + 1) * P], identf[:, :])
                    last.then_inc(xT, 1)

            def hilo(bank, lh, ll, rh, rl):
                n = len(lh)
                for c in range(n):
                    for m, (a, x) in enumerate(((lh[c], rh[c]), (lh[c], rl[c]), (ll[c], rh[c]))):
                        last = nc.tensor.matmul(bank, a, x, start=(c == 0 and m == 0),
                                                stop=(c == n - 1 and m == 2))
                return last

            transpose_x(0)
            pe.wait_ge(wa_split, 1)
            for b in range(BLOCKS):
                if b + 1 < BLOCKS:
                    transpose_x(b + 1)
                pe.wait_ge(xsplit, DC * (b + 1))
                xh = [XTh[:, b % 2, c, :] for c in range(DC)]
                xl = [XTl[:, b % 2, c, :] for c in range(DC)]
                for r in range(4 * b, 4 * b + 4):
                    _, w, half = QK_ROUNDS[r]
                    f = slice(half * P, (half + 1) * P)
                    if r >= 4:
                        pe.wait_ge(rest_ready, r - 3)
                    hilo(psT[:, r % 4, :], [WAh[:, w, c, f] for c in range(DC)],
                         [WAl[:, w, c, f] for c in range(DC)], xh, xl).then_inc(qk_proj, 1)
                for v in range(2 * b, 2 * b + 2):
                    if v >= 2:
                        pe.wait_ge(v_ready, v - 1)
                    if v == 1:
                        pe.wait_ge(cols_ready, 1)
                    for t in range(2):
                        k = slice(((2 * v + t) % TPB) * P, ((2 * v + t) % TPB + 1) * P)
                        last = hilo((psA, psM)[v % 2][:, t * D:(t + 1) * D],
                                    [XTh[:, b % 2, c, k] for c in range(DC)],
                                    [XTl[:, b % 2, c, k] for c in range(DC)],
                                    [WAh[:, 2, c, :] for c in range(DC)],
                                    [WAl[:, 2, c, :] for c in range(DC)])
                    last.then_inc(v_proj, 1)

            pe.wait_ge(rest_ready, len(QK_ROUNDS))
            pe.wait_ge(wffn_in, 48)
            n = 0

            def bank_free(n):
                if n >= 4:
                    pe.wait_ge(prep_evac, n - 3)

            for c in range(DC):
                for q in range(4):
                    bank_free(n)
                    for t in range(4):
                        last = nc.tensor.transpose(psT[:, n % 4, t * P:(t + 1) * P],
                                                   wug_raw[:, 4 * q + t, c * P:(c + 1) * P], identf[:, :])
                    last.then_inc(prep_mm, 1)
                    n += 1
            pe.wait_ge(hadm_ready, 1)
            pe.wait_ge(prep_evac, 2 * 4)
            for c in range(DC):
                for q in range(4):
                    bank_free(n)
                    nc.tensor.matmul(psT[:, n % 4, :], hadp[:, :], WT[:, 0, q * BW:(q + 1) * BW],
                                     start=True, stop=False)
                    nc.tensor.matmul(psT[:, n % 4, :], (hadp, hadm)[c][:, :], WT[:, 1, q * BW:(q + 1) * BW],
                                     start=False, stop=True).then_inc(prep_mm, 1)
                    n += 1
            pe.wait_ge(wd_rot, 1)
            for q in range(4):
                bank_free(n)
                for j in range(2):
                    for c in range(DC):
                        k = 2 * q + j
                        last = nc.tensor.transpose(psT[:, n % 4, j * D + c * P:j * D + (c + 1) * P],
                                                   WDx[:, c, k * P:(k + 1) * P], identf[:, :])
                last.then_inc(prep_mm, 1)
                n += 1
            for q in range(4):
                pe.wait_ge(prep_evac, 16 + q + 1)
                bank_free(n)
                nc.tensor.matmul(psT[:, n % 4, :], hadp[:, :],
                                 WDT[:, 2 * q:2 * q + 2, :].rearrange("p c o -> p (c o)"),
                                 start=True, stop=True).then_inc(prep_mm, 1)
                n += 1
            pe.wait_ge(prep_evac, n)

            def max_bank(i, k, n, bank, par):
                kind, heads, k0, width, _ = max_jobs(i)[k]
                if not (isinstance(n, int) and n < 2):
                    pe.wait_ge(max_done, n - 1)
                if kind == "diag":
                    nc.tensor.matmul(psS[:, bank, :], identb[:, :], mask[:, :, :], start=True, stop=False)
                for m, h in enumerate(heads):
                    last = nc.tensor.matmul(psS[:, bank, m * width:(m + 1) * width],
                                            at(QA, par, slice(0, ROWS), h, slice(i * P, (i + 1) * P)),
                                            at(KA, par, slice(0, ROWS), h, slice(k0, k0 + width)),
                                            start=(kind != "diag"),
                                            stop=(kind != "diag" or m == len(heads) - 1))
                last.then_inc(max_scores, 1)

            def max_rows(b, n, norms):
                pe.wait_ge(mparts_ready, n + 1)
                pe.wait_ge(norm_done, norms + START)
                if not (isinstance(n, int) and n < 1):
                    pe.wait_ge(mrows_ready, n)
                pe.sem_inc(pe_waited, 1)
                nc.tensor.transpose(psMb[0:MROWS * HG * TPB, 0:P],
                                    mparts[:, b % 2, :, :, :].rearrange("p h m t -> p (h m t)"),
                                    identb[:, :]).then_inc(mrowsT, 1)

            n = 0
            pe.wait_ge(consts_ready, 5)
            pe.wait_ge(v_ready, TILES // 2)
            pe.wait_ge(ops_in, 16 * 12)
            for s in FIRST:
                if s[0] == "max":
                    max_bank(s[1], s[2], n, n % 2, 0)
                    n += 1
                elif s[0] == "rowmaxT":
                    max_rows(s[1], s[1], 0)

            def group(g, last):
                units = g * GROUP_UNITS
                par, nxt = pe.snap(g % 2) if not last else g % 2, None
                if not last:
                    nxt = pe.snap((g + 1) % 2)
                n = m = norms = 0
                waited = False
                for s in group_steps(last):
                    if s[0] == "max":
                        ahead = s[1] < LEAD
                        if ahead and not waited:
                            pe.wait_ge(ops_in, (g + 2) * (16 * 12))
                            waited = True
                        max_bank(s[1], s[2], g * GROUP_MAX + FIRST_MAX + n, (FIRST_MAX + n) % 2,
                                 nxt if ahead else par)
                        n += 1
                    elif s[0] == "rowmaxT":
                        max_rows(s[1], g * BLOCKS + FIRST_RM + m, g * BLOCKS + norms)
                        m += 1
                    elif s[0] == "exp":
                        _, b, j = s
                        u = unit_no(b, j)
                        off = max(j - TPB * b, 0) * P
                        if j == 0:
                            pe.wait_ge(mrows_in[b % 2], (g * (BLOCKS // 2) + b // 2 + 1) * (16 * HG))
                        for h in range(HG):
                            if h % 2 == 0:
                                pe.wait_ge(probs, (units + u) * 2 + START + (h // 2 - 1 if u or h else 0))
                            last_mm = nc.tensor.matmul(
                                psT[:, h, off:BW],
                                at(KA, par, slice(0, ROWS + MROWS), h, slice(j * P, (j + 1) * P)),
                                at(QA, par, slice(0, ROWS + MROWS), h, slice(b * BW + off, (b + 1) * BW)),
                                start=True, stop=True)
                            if h % 2 == 1:
                                last_mm.then_inc(scores, 1)
                    elif s[0] == "av":
                        _, b, j = s
                        u = unit_no(b, j)
                        off = max(j - TPB * b, 0) * P
                        if j >= TPB * b:
                            pe.wait_ge(masked, g * TILES + diag_no(b, j))
                        else:
                            pe.wait_ge(probs, (units + u) * 2 + 2 + START)
                        if j == 0:
                            pe.wait_ge(av_out, g * BLOCKS + b + START)
                        if j == TPB * b:
                            pe.wait_ge(vg_ready, g * BLOCKS + b + 1)
                        for h in range(HG):
                            last_mm = nc.tensor.matmul(psA[32 * h:32 * h + 32, off:BW], VG[:, j, h, :],
                                                       PR[:, u % PRING, h, off:BW],
                                                       start=(j == 0), stop=(j == TPB * (b + 1) - 1))
                        last_mm.then_inc(av_done, 1)
                    elif s[0] == "norm":
                        b = s[1]
                        pe.wait_ge(av_out, g * BLOCKS + b + 1 + START)
                        pe.wait_ge(norm_done, g * BLOCKS + norms + START)
                        pe.wait_ge(mrows_ready, g * BLOCKS + FIRST_RM + m)
                        for t in range(TPB):
                            last_mm = nc.tensor.transpose(psM[:, t * P:(t + 1) * P],
                                                          avT[:, b % 2, t * P:(t + 1) * P], identf[:, :])
                        last_mm.then_inc(avT_done, 1)
                        norms += 1

            with pe.Fori(0, GROUPS - 1) as g:
                group(g, False)
            group(GROUPS - 1, True)

            pe.wait_ge(norm_done, GROUPS * BLOCKS + START)
            pe.wait_ge(max_done, FIRST_MAX + GROUP_MAX * GROUPS - FIRST_MAX)

            def transpose_x2(b):
                pe.wait_ge(xh2_ready, b + 1)
                for c in range(DC):
                    if b >= 1:
                        pe.wait_ge(x2_split, DC * (b - 1) + c + 1)
                    for t in range(TPB):
                        last = nc.tensor.transpose(psT[:, 2 + c, t * P:(t + 1) * P],
                                                   xh2[:, b % 2, t, c * P:(c + 1) * P], identf[:, :])
                    last.then_inc(x2T, 1)

            pe.wait_ge(probs, GROUPS * GROUP_UNITS * 2 + START)
            for b in range(BLOCKS):
                for c in range(DC):
                    if b >= 1:
                        pe.wait_ge(oT_split, DC * (b - 1) + c + 1)
                    for t in range(TPB):
                        last = nc.tensor.transpose(psS[:, c, t * P:(t + 1) * P],
                                                   O[:, b * TPB + t, c * P:(c + 1) * P], identf[:, :])
                    last.then_inc(oT, 1)
                if b >= 1:
                    transpose_x2(b - 1)
                pe.wait_ge(oT_split, DC * (b + 1))
                pe.wait_ge(wsplit, 1)
                for v in range(2):
                    if b >= 1:
                        pe.wait_ge(x1_ready, 2 * (b - 1) + v + 1)
                    for t in range(2):
                        k = slice((2 * v + t) * P, (2 * v + t + 1) * P)
                        last = hilo(psT[:, v, t * D:(t + 1) * D],
                                    [OTh[:, c, k] for c in range(DC)], [OTl[:, c, k] for c in range(DC)],
                                    [Woh[:, c, :] for c in range(DC)], [Wol[:, c, :] for c in range(DC)])
                    last.then_inc(o_proj, 1)
            transpose_x2(BLOCKS - 1)
            pe.wait_ge(x2_split, DC * BLOCKS)
            pe.wait_ge(wsplit, 4)

            with pe.Fori(0, BLOCKS) as b:
                def down(k):
                    pe.wait_ge(h_split, b * IC + k + 1)
                    for t in range(TPB):
                        if k == 0:
                            pe.wait_ge(y_ready, b * TPB + START)
                        sl = slice(t * P, (t + 1) * P)
                        for m, (a, x) in enumerate(((Hh, Dh), (Hh, Dl), (Hl, Dh))):
                            last = nc.tensor.matmul(down_bank(t), a[:, k % 4, sl], x[:, k, :],
                                                    start=(k == 0 and m == 0),
                                                    stop=(k == IC - 1 and m == 2))
                    last.then_inc(down_k, 1)

                for k in range(IC):
                    if k >= 2:
                        pe.wait_ge(h_ready, b * IC + k - 1 + START)
                    else:
                        pe.wait_ge(h_ready, b * IC + START)
                    for which in range(2):
                        f = slice((1 - which) * INTER + k * P, (1 - which) * INTER + (k + 1) * P)
                        xs = ds(b * BW, BW)
                        last = hilo(psT[:, 2 * (k % 2) + which, :],
                                    [UGh[:, c, f] for c in range(DC)], [UGl[:, c, f] for c in range(DC)],
                                    [X2h[:, c, xs] for c in range(DC)], [X2l[:, c, xs] for c in range(DC)])
                    last.then_inc(ug_mm, 1)
                    if k >= 2:
                        down(k - 2)
                down(IC - 2)
                down(IC - 1)


_INS = ["L0_attn_X", "L0_attn_ln_g", "L0_attn_ln_b", "L0_attn_Wq", "L0_attn_bq", "L0_attn_Wk",
        "L0_attn_bk", "L0_attn_Wv", "L0_attn_bv", "L0_attn_Wo", "L0_attn_bo", "L0_ffn_SU_ug",
        "L0_ffn_SU_dp", "L0_ffn_Wscale_ug", "L0_ffn_Wscale_dp", "L0_ffn_W_up", "L0_ffn_W_gate",
        "L0_ffn_W_down"]


def kernel(**inputs):
    import numpy as np
    import concourse.bacc as bacc
    from concourse.bass_utils import run_bass_kernel_spmd

    nc = bacc.Bacc("TRN2", target_bir_lowering=False, num_devices=1)
    arrays, args = {}, []
    for name in _INS:
        a = np.ascontiguousarray(inputs[name])
        arrays[name] = a
        args.append(nc.dram_tensor(name, a.shape, mybir.dt.from_np(a.dtype), kind="ExternalInput").ap())
    had = np.ones((1, 1), np.float32)
    while had.shape[0] < P:
        had = np.block([[had, had], [had, -had]])
    arrays["had"] = np.ascontiguousarray(had, np.float32)
    args.append(nc.dram_tensor("had", (P, P), mybir.dt.float32, kind="ExternalInput").ap())
    args.append(nc.dram_tensor("out", (1, SEQ, D), mybir.dt.float32, kind="ExternalOutput").ap())
    build(nc, *args)
    r = run_bass_kernel_spmd(nc, [arrays], core_ids=[0])
    return r.results[0]["out"]
```

```python
import concourse.bass as bass
from concourse import mybir
from contextlib import ExitStack

SEQ, D, HEADS, INTER = 2048, 256, 16, 1024
P = 128
DH = D // HEADS
TILES = SEQ // P
BW = 512
BLOCKS = SEQ // BW
TPB = BW // P
DC = D // P
IC = INTER // P
HG = 4
GROUPS = HEADS // HG
EPS = 1e-5
START = 1
NEG = -1.0e30
LOWEST = -3.0e38
Q_SLOTS = (0, 0, 0, 1, 1, 2)
K_SLOTS = (0, 1, 2, 0, 1, 0)
SLOTS = len(Q_SLOTS)
ROWS = SLOTS * DH
MROWS = 3
NSLOT = 2 + BLOCKS - 1
PRING = 4
AVLAG = 2
C_G, C_B, C_BQ, C_BK, C_SUG, C_SDP, C_WUG, C_WDP = 0, 2, 4, 6, 8, 10, 18, 34
NCOLS = 36

EH = 2
SRING = 3
TRING = 4 // EH
PREP_ROUNDS = 24


def max_jobs(i):
    full, rem = divmod(i, TPB)
    jobs = [("diag", (0, 1, 2, 3), i * P, P, 0)]
    per = BW // (rem * P) if rem else 0
    for h in range(0, HG, per) if rem else ():
        jobs.append(("part", tuple(range(h, h + per)), full * BW, rem * P, 1))
    for f in range(full):
        for h in range(HG):
            jobs.append(("part", (h,), f * BW, BW, 2 + f))
    return jobs


UNITS = sum(TPB * (b + 1) for b in range(BLOCKS))


def unit_no(g, b, j):
    return g * UNITS + sum(TPB * (x + 1) for x in range(b)) + j


def is_diag(b, j):
    return j >= TPB * b


def plan():
    TO_READER, TO_PE = 0.18, 0.08
    t = dve = act = 0.0
    steps = []
    maxq = []
    for g in range(GROUPS):
        for i in range(TILES):
            maxq += [("max", g, i, k) for k in range(len(max_jobs(i)))]
            if i % TPB == TPB - 1:
                maxq.append(("rowmax", g, i // TPB))
    units = [(g, b, j) for g in range(GROUPS) for b in range(BLOCKS) for j in range(TPB * (b + 1))]
    expq = [u + (h,) for u in units for h in range(0, HG, EH)]
    avq = list(units)
    prepq = list(range(PREP_ROUNDS))
    s_read, t_read, av_at = [], [], {}
    rows_at, exp_at, later = {}, {}, []
    ops_at = {0: 0.0, 1: 8.0}
    psA_free, chain_block = 0.0, 0

    def s_free():
        return s_read[-SRING] if len(s_read) >= SRING else 0.0

    def t_free():
        return t_read[-TRING] if len(t_read) >= TRING else 0.0

    while maxq or expq or avq or later or prepq:
        cand = []
        for n, (r, st) in enumerate(later):
            if st[0] == "oT" and st[1] != chain_block:
                continue
            cand.append((r if st[0] == "xh2" else max(r, s_free()), 0, "later", n))
        if maxq and maxq[0][1] in ops_at:
            cand.append((max(s_free(), ops_at[maxq[0][1]]), 1, "max", 0))
        if avq and avq[0] in exp_at:
            g, b, j = avq[0]
            cand.append((max(exp_at[avq[0]], psA_free if j == 0 else 0.0), 2, "av", 0))
        if expq:
            g, b, j, h = expq[0]
            u = unit_no(g, b, j)
            if (g, b) in rows_at and (u < PRING or u - PRING in av_at) and not (g == GROUPS - 1 and prepq):
                cand.append((max(t_free(), rows_at[g, b], av_at.get(u - PRING, 0.0)), 1.5, "exp", 0))
        if prepq:
            if prepq[0] < 16 or expq[0] > (0, 3, 0, 0):
                cand.append((t_free(), 4, "prep", 0))
        now = [c for c in cand if c[0] <= t]
        r, _, kind, n = min(now, key=lambda c: c[1]) if now else min(cand)
        t = max(t, r)
        if kind == "max":
            st = maxq.pop(0)
            steps.append(st)
            what, heads, _, width, _ = max_jobs(st[2])[st[3]]
            cols = len(heads) * width
            t += cols * (2 if what == "diag" else 1) / 2400
            dve = max(dve, t + TO_READER) + cols / 960 + 0.07
            s_read.append(dve + TO_PE)
            if maxq and maxq[0][0] == "rowmax":
                st = maxq.pop(0)
                steps.append(st)
                dve += 0.4
                later.append((dve + 3.0, ("rowmaxT",) + st[1:]))
        elif kind == "exp":
            g, b, j, h = expq.pop(0)
            w = BW - max(j - TPB * b, 0) * P
            t += EH * w / 2400
            steps.append(("exp", g, b, j, h))
            act = max(act, t + TO_READER) + EH * w / 1200 + 0.06
            t_read.append(act + TO_PE)
            if h + EH == HG:
                exp_at[g, b, j] = act + TO_PE + (1.2 if is_diag(b, j) else 0.0)
        elif kind == "av":
            g, b, j = avq.pop(0)
            w = BW - max(j - TPB * b, 0) * P
            t += 4 * w / 2400 + 0.08
            steps.append(("av", g, b, j))
            av_at[unit_no(g, b, j)] = t + 0.1
            if j == TPB * (b + 1) - 1:
                steps.append(("avout", g, b))
                act = max(act, t + TO_READER) + 0.5
                psA_free = act + TO_PE
                later.append((psA_free, ("norm", g, b)))
                if b == BLOCKS - 1:
                    ops_at[g + 2] = t + 12.0
        elif kind == "prep":
            n = prepq.pop(0)
            steps.append(("prep", n))
            t += 0.25 if n < 8 or 16 <= n < 20 else 1.7
            act = max(act, t + TO_READER) + 0.5
            t_read.append(act + TO_PE)
        else:
            st = later.pop(n)[1]
            b = st[-1]
            if st[0] == "xh2":
                steps.append(st)
                dve += 1.6
                later.append((dve + 0.2, ("x2T", b)))
            elif st[0] in ("rowmaxT", "norm"):
                steps.append(st)
                t += 0.06 if st[0] == "rowmaxT" else 0.22
                dve = max(dve, t + TO_READER) + (0.3 if st[0] == "rowmaxT" else 0.8)
                s_read.append(dve + TO_PE)
                if st[0] == "rowmaxT":
                    rows_at[st[1:]] = dve + 2.5
                elif st[1] == GROUPS - 1:
                    later.append((dve + 0.2, ("oT", b)))
            else:
                for c in range(2):
                    steps.append((st[0], b, c))
                    t = max(t, s_free()) + (1.3 if st[0] == "oproj" else 0.25)
                    dve = max(dve, t + TO_READER + (0.0 if st[0] == "oproj" else 0.6)) + 0.6
                    s_read.append(dve + TO_PE)
                if st[0] == "oT":
                    later.append((dve + 0.2, ("oproj", b)))
                elif st[0] == "oproj":
                    dve += 2.0
                    later.append((dve + 4.0, ("xh2", b)))
                else:
                    chain_block += 1
    return steps


ORDER = plan()
S_STEPS = [s for s in ORDER if s[0] in ("max", "rowmaxT", "norm", "oT", "oproj", "x2T")]
T_STEPS = [s for s in ORDER if s[0] in ("exp", "prep")]
S_NO = {s: n for n, s in enumerate(S_STEPS)}
T_NO = {s: n for n, s in enumerate(T_STEPS)}


def t_done(g, b, j):
    return T_NO["exp", g, b, j, HG - EH] + 1


def diag_no(g, b, j):
    return g * TILES + j + 1


def build(nc, X, ln_g, ln_b, Wq, bq, Wk, bk, Wv, bv, Wo, bo, SU_ug, SU_dp, Ws_ug, Ws_dp,
          W_up, W_gate, W_down, had, out):
    f32, bf16, f32r = mybir.dt.float32, mybir.dt.bfloat16, mybir.dt.float32r
    ALU = mybir.AluOpType
    ACT = mybir.ActivationFunctionType
    AX = mybir.AxisListType
    ds = bass.ds

    nc.disable_value_cache = True
    ctx = ExitStack()
    with ctx:
        sem_of = {}

        def sem(name):
            sem_of[name] = ctx.enter_context(nc.semaphore(name))
            return sem_of[name]

        size = {f32: 4, f32r: 4, bf16: 2}
        top = [(nc.sbuf_base + 63) // 64 * 64]

        def area(nbytes):
            at = top[0]
            top[0] += (nbytes + 63) // 64 * 64
            return at

        def put(name, shape, dt, at=None):
            n = size[dt]
            for s in shape[1:]:
                n *= s
            if at is None:
                at = area(n)
            return nc.alloc_sbuf_tensor_at(name, shape, dt, offset=at), at + n

        def sb(name, shape, dt):
            return put(name, shape, dt)[0]

        identf = sb("identf", [P, P], f32)
        identb = sb("identb", [P, P], bf16)
        mask = sb("mask", [P, HG, P], bf16)
        hadp = sb("hadp", [P, P], f32)
        hadm = sb("hadm", [P, P], f32)
        rows = sb("rows", [NCOLS, P], f32)
        cols = sb("cols", [P, NCOLS], f32)
        bv_all = sb("bv_all", [P, D], f32)
        bo_all = sb("bo_all", [P, D], f32)
        stats = sb("stats", [P, TILES, 6], f32)
        meanvar = sb("meanvar", [P, TILES, 2], f32)
        halves = sb("halves", [P, TILES], f32)
        var_eps = sb("var_eps", [P, TILES], f32)
        rstd = sb("rstd", [P, TILES], f32)
        lnshift = sb("lnshift", [P, TILES], f32)
        pmax = sb("pmax", [P, 2, TPB, HG, NSLOT], f32)
        negmax = sb("negmax", [P, 2, TPB * HG], f32)
        mrest = sb("mrest", [P, 2, TPB * HG], f32)
        mparts = sb("mparts", [P, 2, HG, MROWS, TPB], bf16)
        mrows = sb("mrows", [MROWS * HG * TPB, 2, P], bf16)
        recip = sb("recip", [P, 2, TPB * HG], f32)

        a_ops = area(2 * 2 * HG * SEQ * 2)
        QA, _ = put("QA", [P, 2, HG, SEQ], bf16, a_ops)
        KA, _ = put("KA", [P, 2, HG, SEQ], bf16, a_ops + 2 * HG * SEQ * 2)
        a_v = area(TILES * D * 4)
        V, _ = put("V", [P, TILES, D], f32, a_v)
        a_vg = area(TILES * HG * 32 * 4)
        VG, _ = put("VG", [P, TILES, HG, 32], f32, a_vg)
        a_pr = area(PRING * HG * BW * 4)
        PR, _ = put("PR", [P, PRING, HG, BW], f32, a_pr)
        avT = sb("avT", [P, 2, BW], f32)
        a_o = area(TILES * D * 4)
        xin, _ = put("xin", [P, TILES, D], f32, a_o)
        O, _ = put("O", [P, TILES, D], f32, a_o)
        WUG = sb("WUG", [P, 2 * IC * D], f32)
        WD = sb("WD", [P, IC * D], f32)
        a_e = area(32 * 1024)
        assert top[0] <= nc.sbuf_usable_end, (top[0], nc.sbuf_usable_end)

        XTh, n = put("XTh", [P, 2, DC, BW], f32r, a_e)
        XTl, n = put("XTl", [P, 2, DC, BW], f32r, n)
        xnf, n = put("xnf", [P, 2, BW], f32, n)
        WAh, n = put("WAh", [P, 3, DC, D], f32r, n)
        WAl, n = put("WAl", [P, 3, DC, D], f32r, n)
        wa_raw, _ = put("wa_raw", [P, 3, DC, D], f32, a_vg)
        second = a_ops + HG * SEQ * 2
        parts, n = put("parts", [P, 3, 3, BW], bf16, second)
        part_rest, n = put("part_rest", [P, 2, BW], f32, n)
        assert n <= second + HG * SEQ * 2
        WT, n = put("WT", [P, DC, 2 * INTER], f32, a_e)
        WDx, n = put("WDx", [P, DC, INTER], f32, n)
        WDT, n = put("WDT", [P, IC, D], f32, n)
        assert n <= a_e + 32 * 1024
        ones, _ = put("ones", [MROWS, SEQ], bf16, a_pr)
        wug_raw = WUG[:, :].rearrange("p (t f) -> p t f", f=D)
        wug = WUG[:, :].rearrange("p (c o) -> p c o", c=DC)
        wd_raw = WD[:, :].rearrange("p (c i) -> p c i", c=DC)
        wd = WD[:, :].rearrange("p (c o) -> p c o", c=IC)

        quarter = HG * SEQ * 2
        X1, _ = put("X1", [P, TILES, D], f32, a_ops)
        Dh, n = put("Dh", [P, IC, D], f32r, a_ops + quarter)
        Dl, _ = put("Dl", [P, IC, D], f32r, n)
        X2h, _ = put("X2h", [P, DC, SEQ], f32r, a_ops + 2 * quarter)
        Hh, n = put("Hh", [P, 4, BW], f32r, a_ops + 3 * quarter)
        Hl, _ = put("Hl", [P, 4, BW], f32r, n)
        X2l, _ = put("X2l", [P, DC, SEQ], f32r, a_v)
        UGh, n = put("UGh", [P, DC, 2 * INTER], f32r, a_pr)
        UGl, _ = put("UGl", [P, DC, 2 * INTER], f32r, n)
        wo_raw, n = put("wo_raw", [P, DC, D], f32, a_e)
        Woh, n = put("Woh", [P, DC, D], f32r, n)
        Wol, n = put("Wol", [P, DC, D], f32r, n)
        OTh, n = put("OTh", [P, DC, BW], f32r, n)
        OTl, n = put("OTl", [P, DC, BW], f32r, n)
        xh2, n = put("xh2", [P, TPB, D], f32, n)
        sg, n = put("sg", [P, 2, BW], f32, n)
        hf, n = put("hf", [P, 2, BW], f32, n)
        yst, n = put("yst", [P, TPB, D], f32, n)
        assert n <= a_e + 32 * 1024

        psS = ctx.enter_context(nc.psum_tensor("psS", [P, SRING, BW], f32))
        psT = ctx.enter_context(nc.psum_tensor("psT", [P, 4, BW], f32))
        psA = ctx.enter_context(nc.psum_tensor("psA", [P, BW], f32))
        psM = psS[:, SRING - 1, :]

        scr = nc.dram_tensor("scr", (2, 3, D, SEQ), bf16, kind="Internal").ap()

        x_in = [sem(f"x_in{b}") for b in range(BLOCKS)]
        rows_in, wa_in, bias_in, had_in, wffn_in = (sem(n) for n in
            ("rows_in", "wa_in", "bias_in", "had_in", "wffn_in"))
        dve_link, pool_link = sem("dve_link"), sem("pool_link")
        consts_ready, halves_ready = sem("consts_ready"), sem("halves_ready")
        hadm_ready = sem("hadm_ready")
        rowsT, cols_ready = sem("rowsT"), sem("cols_ready")
        var_ready, rstd_ready, xh_ready = sem("var_ready"), sem("rstd_ready"), sem("xh_ready")
        xT, xnf_ready, xsplit = sem("xT"), sem("xnf_ready"), sem("xsplit")
        wa_split = sem("wa_split")
        qk_proj, part0, bank_read, rest_ready, parts_ready = (sem(n) for n in
            ("qk_proj", "part0", "bank_read", "rest_ready", "parts_ready"))
        scr_out = [sem(f"scr_out{i}") for i in range(3)]
        v_proj, v_ready = sem("v_proj"), sem("v_ready")
        ops0_in = [sem(f"ops0_in{b}") for b in range(BLOCKS)]
        ops_in, ones_ready, ones_in = sem("ops_in"), sem("ones_ready"), sem("ones_in")
        wa_hi = sem("wa_hi")
        wd_rot = sem("wd_rot")
        vg_ready = sem("vg_ready")
        s_filled, s_read, t_filled, t_read = (sem(n) for n in ("s_filled", "s_read", "t_filled", "t_read"))
        rowmax_ready, mparts_ready, mrows_ready = (sem(n) for n in
            ("rowmax_ready", "mparts_ready", "mrows_ready"))
        mrows_in = [sem(f"mrows_in{i}") for i in range(2)]
        masked, av_done, av_out, recip_ready = (sem(n) for n in
            ("masked", "av_done", "av_out", "recip_ready"))
        xre_in, wo_in, xb_ready, wsplit_hi, wsplit = (sem(n) for n in
            ("xre_in", "wo_in", "xb_ready", "wsplit_hi", "wsplit"))
        oT_hi, var2, rstd2, xh2_ready, x2_hi = (sem(n) for n in
            ("oT_hi", "var2", "rstd2", "xh2_ready", "x2_hi"))
        ug_mm, silu_ready, h_ready, h_hi, h_split, down_k, y_ready, y_out = (sem(n) for n in
            ("ug_mm", "silu_ready", "h_ready", "h_hi", "h_split", "down_k", "y_ready", "y_out"))

        block = ctx.enter_context(nc.Block())

        QK_ROUNDS = [(b, w, half) for b in range(BLOCKS) for w in range(2) for half in range(DC)]

        def down_bank(t):
            return (psS[:, 0, 0:D], psS[:, 1, 0:D], psA[:, 0:D], psM[:, 0:D])[t]

        def ug_chunk(w, c, k):
            return w[:, c, :].rearrange("p (g k o) -> p g k o", g=2, o=P)[:, :, k, :]

        @block.sync
        def _(sp):
            sp.sem_inc(y_out, START)
            x_t = X.rearrange("a (t p) f -> p (a t) f", p=P)

            def load_x(b):
                sp.dma_start(xin[:, b * TPB:(b + 1) * TPB, :],
                             x_t[:, b * TPB:(b + 1) * TPB, :]).then_inc(x_in[b], 16)

            load_x(0)
            for w, src in enumerate((Wq, Wk, Wv)):
                sp.dma_start(wa_raw[:, w, :, :], src.rearrange("(c p) n -> p c n", p=P)).then_inc(wa_in, 16)
            load_x(1)
            for c, v in ((C_G, ln_g), (C_B, ln_b), (C_BQ, bq), (C_BK, bk), (C_SUG, SU_ug),
                         (C_SDP, SU_dp), (C_WUG, Ws_ug), (C_WDP, Ws_dp)):
                v = v.rearrange("(c p) -> c p", p=P)
                sp.dma_start(rows[c:c + v.shape[0], :], v).then_inc(rows_in, 16)
            load_x(2)
            load_x(3)
            for dst, src in ((bv_all, bv), (bo_all, bo)):
                sp.dma_start(dst[:, :], src.rearrange("(a n) -> a n", a=1).to_broadcast([P, D]))\
                  .then_inc(bias_in, 16)
            sp.dma_start(hadp[:, :], had).then_inc(had_in, 16)
            sp.wait_ge(ones_ready, 1)
            for par in range(2):
                for h in range(HG):
                    sp.dma_start(KA[ROWS:ROWS + MROWS, par, h, :], ones[:, :]).then_inc(ones_in, 16)
            for n, src in enumerate((W_up, W_gate)):
                sp.dma_start(wug_raw[:, n * IC:(n + 1) * IC, :],
                             src.rearrange("(t o) f -> o t f", o=P)).then_inc(wffn_in, 16)
            sp.dma_start(wd_raw, W_down.rearrange("(c o) i -> o c i", o=P)).then_inc(wffn_in, 16)

            def load_ops(g, toks, signal, slots=range(SLOTS)):
                for i in slots:
                    for w, dst, part in ((0, QA, Q_SLOTS[i]), (1, KA, K_SLOTS[i])):
                        src = scr[w, part, g * HG * DH:(g + 1) * HG * DH, toks].rearrange("(h d) n -> d h n", d=DH)
                        sp.dma_start(dst[i * DH:(i + 1) * DH, g % 2, :, toks], src).then_inc(signal, 16)

            def load_block(b, slots):
                if slots[0] == 0:
                    for i in range(3):
                        sp.wait_ge(scr_out[i], 16 * len(QK_ROUNDS[:4 * b + 4][i::3]))
                load_ops(0, slice(b * BW, (b + 1) * BW), ops0_in[b], slots)

            for b in range(BLOCKS):
                for r in range(4 * b, 4 * b + 4):
                    _, w, half = QK_ROUNDS[r]
                    sp.wait_ge(parts_ready, r + 1)
                    sp.dma_start(scr[w, :, half * P:(half + 1) * P, b * BW:(b + 1) * BW]
                                 .rearrange("s f n -> f s n"), parts[:, r % 3, :, :]).then_inc(scr_out[r % 3], 16)
                    if b and r % 4:
                        load_block(b - 1, range(r % 4 * 2 - 2, r % 4 * 2))
            load_block(BLOCKS - 1, range(SLOTS))

            load_ops(1, slice(0, SEQ), ops_in)

            for s in ORDER:
                if s[0] == "rowmaxT":
                    _, g, b = s
                    sp.wait_ge(mrows_ready, g * BLOCKS + b + 1)
                    for h in range(HG):
                        dst = QA[ROWS:ROWS + MROWS, g % 2, h, b * BW:(b + 1) * BW]\
                            .rearrange("m (t q) -> m t q", t=TPB)
                        sp.dma_start(dst, mrows[h * MROWS * TPB:(h + 1) * MROWS * TPB, b % 2, :])\
                          .then_inc(mrows_in[b % 2], 16)
                elif s[0] == "avout" and s[2] == BLOCKS - 1:
                    g = s[1]
                    sp.wait_ge(av_done, (g + 1) * UNITS)
                    if g + 2 < GROUPS:
                        sp.wait_ge(ops_in, (g + 1) * (16 * 2 * SLOTS))
                        load_ops(g + 2, slice(0, SEQ), ops_in)
                    elif g == GROUPS - 2:
                        sp.dma_start(X1[:, :, :], x_t).then_inc(xre_in, 16)
                        sp.wait_ge(t_read, T_NO["prep", PREP_ROUNDS - 1] + 1)
                        sp.dma_start(wo_raw[:, :, :], Wo.rearrange("(c p) n -> p c n", p=P)).then_inc(wo_in, 16)

            out_t = out.rearrange("a (t p) f -> p (a t) f", p=P)
            with sp.Fori(0, BLOCKS) as b:
                sp.wait_ge(y_ready, b * TPB + TPB + START)
                sp.dma_start(out_t[:, ds(b * TPB, TPB), :], yst[:, :, :]).then_inc(y_out, 16)
            sp.wait_ge(y_out, 16 * BLOCKS + START)

        @block.gpsimd
        def _(pool):
            chain = [0]

            def link(ins):
                chain[0] += 1
                ins.then_inc(pool_link, 1)
                pool.wait_ge(pool_link, chain[0])

            nc.gpsimd.memset(halves[:, :], -0.5).then_inc(halves_ready, 1)
            nc.gpsimd.memset(identf[:, :], 0.0)
            nc.gpsimd.memset(identb[:, :], 0.0)
            link(nc.gpsimd.memset(mask[:, :, :], 0.0))
            nc.gpsimd.affine_select(out=identf[:, :], in_=identf[:, :], compare_op=ALU.not_equal, fill=1.0,
                                    base=0, pattern=[[-1, P]], channel_multiplier=1).then_inc(consts_ready, 1)
            nc.gpsimd.affine_select(out=identb[:, :], in_=identb[:, :], compare_op=ALU.not_equal, fill=1.0,
                                    base=0, pattern=[[-1, P]], channel_multiplier=1).then_inc(consts_ready, 1)
            nc.gpsimd.affine_select(out=mask[:, :, :], in_=mask[:, :, :], compare_op=ALU.is_ge, fill=NEG,
                                    base=0, pattern=[[0, HG], [-1, P]], channel_multiplier=1)\
                .then_inc(consts_ready, 1)
            nc.gpsimd.memset(pmax[:, :, :, :, :], LOWEST).then_inc(consts_ready, 1)

            pool.wait_ge(consts_ready, 4)
            nc.gpsimd.memset(ones[:, :], 1.0).then_inc(ones_ready, 1)
            pool.wait_ge(ones_ready, 1)
            for n, ts in ((1, slice(0, TPB)), (BLOCKS, slice(TPB, TILES))):
                pool.wait_ge(var_ready, n)
                nc.gpsimd.tensor_tensor(out=rstd[:, ts], in0=var_eps[:, ts], in1=halves[:, ts],
                                        op=ALU.pow).then_inc(rstd_ready, 1)
            pool.wait_ge(wa_split, 1)
            link(nc.gpsimd.memset(VG[:, :, :, :], 1.0))
            pool.wait_ge(had_in, 16)
            nc.gpsimd.tensor_scalar(hadm[:, :], hadp[:, :], -1.0, None, ALU.mult).then_inc(hadm_ready, 1)

            for r in range(len(QK_ROUNDS)):
                pool.wait_ge(rest_ready, r + 1)
                nc.gpsimd.tensor_tensor(out=parts[:, r % 3, 2, :], in0=part_rest[:, r % 2, :],
                                        in1=parts[:, r % 3, 1, :], op=ALU.subtract).then_inc(parts_ready, 1)

            def load_vg(g, c):
                src = V[:, c * TPB:(c + 1) * TPB, g * HG * DH:(g + 1) * HG * DH]\
                    .rearrange("p t (h d) -> p t h d", d=DH)
                nc.gpsimd.tensor_copy(VG[:, c * TPB:(c + 1) * TPB, :, 0:DH], src).then_inc(vg_ready, 1)

            for c in range(BLOCKS):
                pool.wait_ge(v_ready, 2 * (c + 1))
                load_vg(0, c)

            def split_max(g, b):
                n = g * BLOCKS + b
                pool.wait_ge(rowmax_ready, n + 1)
                if n >= 2:
                    pool.wait_ge(s_filled, S_NO["rowmaxT", (n - 2) // BLOCKS, (n - 2) % BLOCKS] + 1)
                k = b % 2
                part = [mparts[:, k, :, m, :] for m in range(MROWS)]
                whole, rest = (x[:, k, :].rearrange("p (h t) -> p h t", h=HG) for x in (negmax, mrest))
                link(nc.gpsimd.tensor_copy(part[0], whole))
                link(nc.gpsimd.tensor_tensor(out=rest, in0=whole, in1=part[0], op=ALU.subtract))
                link(nc.gpsimd.tensor_copy(part[1], rest))
                nc.gpsimd.tensor_tensor(out=part[2], in0=rest, in1=part[1],
                                        op=ALU.subtract).then_inc(mparts_ready, 1)

            def rotate_down(n):
                if n < DC:
                    if n == 0:
                        pool.wait_ge(wffn_in, 48)
                        pool.wait_ge(cols_ready, 1)
                        pool.wait_ge(v_proj, TILES // 2)
                    link(nc.gpsimd.tensor_scalar(wd_raw[:, n, :], wd_raw[:, n, :],
                                                 cols[:, C_WDP + n:C_WDP + n + 1],
                                                 float(INTER) ** -0.5, ALU.mult, ALU.mult))
                    return
                step, half = divmod(n - DC, 2)
                w = P << step
                a, o = (x.rearrange("p c (m two w) -> p (c m) two w", two=2, w=w)
                        for x in ((wd_raw, WDx[:, :, :]) if step % 2 == 0 else (WDx[:, :, :], wd_raw)))
                ins = nc.gpsimd.tensor_tensor(out=o[:, :, half, :], in0=a[:, :, 0, :], in1=a[:, :, 1, :],
                                              op=(ALU.add, ALU.subtract)[half])
                if n < DC + 5:
                    link(ins)
                else:
                    ins.then_inc(wd_rot, 1)

            rotation = [(0, b, j) for b in (1, 2) for j in range(TPB)]

            for s in ORDER:
                if s[0] == "rowmax":
                    split_max(*s[1:])
                elif s[0] == "exp" and s[1:4] in rotation and s[4] == 0:
                    rotate_down(rotation.index(s[1:4]))
                elif s[0] == "exp" and is_diag(s[2], s[3]) and s[4] == HG - EH:
                    _, g, b, j, _ = s
                    off = (j - TPB * b) * P
                    pool.wait_ge(t_read, t_done(g, b, j))
                    v = PR[:, unit_no(g, b, j) % PRING, :, off:off + P]
                    nc.gpsimd.affine_select(out=v, in_=v, compare_op=ALU.is_ge, fill=0.0, base=0,
                                            pattern=[[0, HG], [1, P]], channel_multiplier=-1)\
                        .then_inc(masked, 1)
                elif s[0] == "av" and s[2] == BLOCKS - 1 and s[3] % TPB == TPB - 1 and s[1] < GROUPS - 1:
                    pool.wait_ge(av_done, unit_no(*s[1:]) + 1)
                    load_vg(s[1] + 1, s[3] // TPB)
                elif s[0] == "norm" and s[1] == GROUPS - 1:
                    pool.wait_ge(xre_in, 16)
                    v = X1[:, s[2] * TPB:(s[2] + 1) * TPB, :]
                    nc.gpsimd.tensor_tensor(out=v, in0=v, in1=bo_all[:, :].unsqueeze(1)
                                            .to_broadcast([P, TPB, D]), op=ALU.add).then_inc(xb_ready, 1)
                elif s[0] == "oproj" and s[2]:
                    k = s[1] * TPB
                    pool.wait_ge(var2, s[1] + 1)
                    nc.gpsimd.tensor_tensor(out=rstd[:, k:k + TPB], in0=var_eps[:, k:k + TPB],
                                            in1=halves[:, k:k + TPB], op=ALU.pow).then_inc(rstd2, 1)

        @block.scalar
        def _(act):
            act.sem_inc(h_hi, START)
            act.wait_ge(wa_in, 48)
            nc.scalar.activation(WAh[:, :, :, :], wa_raw[:, :, :, :], ACT.Copy).then_inc(wa_hi, 1)
            act.wait_ge(cols_ready, 1)

            def norm_x(b):
                for c in range(DC):
                    n = b * DC + c
                    act.wait_ge(xT, n + 1)
                    if n >= 2:
                        act.wait_ge(xsplit, n - 1)
                    nc.scalar.activation(xnf[:, n % 2, :], psS[:, n % 2, :], ACT.Identity,
                                         bias=cols[:, C_B + c:C_B + c + 1],
                                         scale=cols[:, C_G + c:C_G + c + 1]).then_inc(xnf_ready, 1)

            norm_x(0)
            for b in range(BLOCKS):
                for r in range(4 * b, 4 * b + 4):
                    if r % 4 == 2 and b + 1 < BLOCKS:
                        norm_x(b + 1)
                    _, w, half = QK_ROUNDS[r]
                    c = (C_BQ, C_BK)[w] + half
                    act.wait_ge(qk_proj, r + 1)
                    if r >= 3:
                        act.wait_ge(scr_out[r % 3], 16 * (r // 3))
                    nc.scalar.activation(parts[:, r % 3, 0, :], psT[:, r % 4, :], ACT.Identity,
                                         bias=cols[:, c:c + 1]).then_inc(part0, 1)

            def prep_out(n):
                q, bank = n % 4, psT[:, T_NO["prep", n] % TRING * EH, :]
                act.wait_ge(t_filled, T_NO["prep", n] + 1)
                if n < 16:
                    c = n // 4 % 2
                    dst, scale = (WT, float(D) ** -0.5) if n < 8 else \
                        (wug, cols[:, C_SUG + c:C_SUG + c + 1])
                    if n == 0:
                        act.wait_ge(v_proj, TILES // 2)
                    nc.scalar.activation(dst[:, c, q * BW:(q + 1) * BW], bank, ACT.Copy,
                                         scale=scale).then_inc(t_read, 1)
                elif n < 20:
                    nc.scalar.activation(WDT[:, 2 * q:2 * q + 2, :].rearrange("p c o -> p (c o)"),
                                         bank, ACT.Copy).then_inc(t_read, 1)
                else:
                    for j in range(2):
                        c = 2 * q + j
                        last = nc.scalar.activation(wd[:, c, :], bank[:, j * D:(j + 1) * D], ACT.Copy,
                                                    scale=cols[:, C_SDP + c:C_SDP + c + 1])
                    last.then_inc(t_read, 1)

            def hi_from_psum(s, done, dst, where):
                act.wait_ge(s_filled, S_NO[s] + 1)
                nc.scalar.activation(dst[:, s[2], where], psS[:, S_NO[s] % SRING, :], ACT.Copy)\
                    .then_inc(done, 1)

            for s in ORDER:
                if s[0] == "prep":
                    prep_out(s[1])
                elif s[0] == "exp":
                    _, g, b, j, h = s
                    u = unit_no(g, b, j)
                    off = max(j - TPB * b, 0) * P
                    slot = T_NO[s] % TRING * EH
                    act.wait_ge(t_filled, T_NO[s] + 1)
                    if h == 0 and u >= PRING:
                        act.wait_ge(av_done, u + 1 - PRING)
                    nc.scalar.activation(PR[:, u % PRING, h:h + EH, off:BW], psT[:, slot:slot + EH, off:BW],
                                         ACT.Exp, scale=float(DH) ** -0.5).then_inc(t_read, 1)
                elif s[0] == "avout":
                    _, g, b = s
                    n = g * BLOCKS + b
                    act.wait_ge(av_done, unit_no(g, b, TPB * (b + 1) - 1) + 1)
                    if n >= 2:
                        act.wait_ge(s_filled, S_NO["norm", (n - 2) // BLOCKS, (n - 2) % BLOCKS] + 1)
                    nc.scalar.activation(avT[:, b % 2, :], psA[:, :], ACT.Copy).then_inc(av_out, 1)
                elif s[0] == "norm" and s[1:] == (GROUPS - 1, 0):
                    act.wait_ge(wo_in, 16)
                    nc.scalar.activation(Woh[:, :, :], wo_raw[:, :, :], ACT.Copy).then_inc(wsplit_hi, 1)
                elif s[0] == "oT":
                    hi_from_psum(s, oT_hi, OTh, slice(0, BW))
                elif s[0] == "x2T":
                    hi_from_psum(s, x2_hi, X2h, slice(s[1] * BW, (s[1] + 1) * BW))

            act.wait_ge(av_done, GROUPS * UNITS)
            for k in range(IC):
                for c in range(DC):
                    last = nc.scalar.activation(ug_chunk(UGh, c, k), ug_chunk(wug, c, k), ACT.Copy)
                last.then_inc(wsplit_hi, 1)
                if k == 1:
                    nc.scalar.activation(Dh[:, :, :], wd, ACT.Copy).then_inc(wsplit_hi, 1)

            with act.Fori(0, BLOCKS) as b:
                for k in range(IC):
                    act.wait_ge(ug_mm, b * IC + k + 1)
                    if k >= 2:
                        act.wait_ge(h_ready, b * IC + k - 1 + START)
                    else:
                        act.wait_ge(h_ready, b * IC + START)
                    nc.scalar.activation(sg[:, k % 2, :], psT[:, 2 * (k % 2), :], ACT.Silu,
                                         scale=cols[:, C_WUG + IC + k:C_WUG + IC + k + 1])\
                        .then_inc(silu_ready, 1)
                    act.wait_ge(h_ready, b * IC + k + 1 + START)
                    if k >= 4:
                        act.wait_ge(down_k, b * IC + k - 3 + START)
                    else:
                        act.wait_ge(down_k, b * IC + START)
                    nc.scalar.activation(Hh[:, k % 4, :], hf[:, k % 2, :], ACT.Copy).then_inc(h_hi, 1)

        @block.vector
        def _(dve):
            for s in (h_ready, y_ready):
                dve.sem_inc(s, START)
            chain = [0]

            def link(ins):
                chain[0] += 1
                ins.then_inc(dve_link, 1)
                dve.wait_ge(dve_link, chain[0])

            def x_stats(b):
                ts = range(b * TPB, (b + 1) * TPB)
                dve.wait_ge(x_in[b], 16)
                for t in ts:
                    last = nc.vector.bn_stats(stats[:, t, :], xin[:, t, :])
                link(last)
                for t in ts:
                    last = nc.vector.bn_aggr(meanvar[:, t, :], stats[:, t, :])
                link(last)
                nc.vector.tensor_scalar(var_eps[:, ts.start:ts.stop], meanvar[:, ts.start:ts.stop, 1],
                                        1.0 + EPS, EPS * EPS, ALU.mult, ALU.add).then_inc(var_ready, 1)

            def x_shift(ts, n):
                dve.wait_ge(rstd_ready, n)
                link(nc.vector.scalar_tensor_tensor(out=lnshift[:, ts], in0=meanvar[:, ts, 0], scalar=-1.0,
                                                    in1=rstd[:, ts], op0=ALU.mult, op1=ALU.mult))

            def scale_x(b):
                for t in range(b * TPB, (b + 1) * TPB):
                    nc.vector.tensor_scalar(xin[:, t, :], xin[:, t, :], rstd[:, t:t + 1],
                                            lnshift[:, t:t + 1], ALU.mult, ALU.add).then_inc(xh_ready, 1)

            def split_x(b):
                for c in range(DC):
                    n = b * DC + c
                    dve.wait_ge(xnf_ready, n + 1)
                    if b >= 2:
                        dve.wait_ge(v_proj, 2 * (b - 1))
                    link(nc.vector.tensor_copy(XTh[:, b % 2, c, :], xnf[:, n % 2, :]))
                    nc.vector.tensor_tensor(out=XTl[:, b % 2, c, :], in0=xnf[:, n % 2, :],
                                            in1=XTh[:, b % 2, c, :].bitcast(f32),
                                            op=ALU.subtract).then_inc(xsplit, 1)

            x_stats(0)
            dve.wait_ge(wa_hi, 1)
            nc.vector.tensor_tensor(out=WAl[:, :, :, :], in0=wa_raw[:, :, :, :],
                                    in1=WAh[:, :, :, :].bitcast(f32), op=ALU.subtract).then_inc(wa_split, 1)
            x_shift(slice(0, TPB), 1)
            scale_x(0)
            x_stats(1)
            dve.wait_ge(rowsT, 1)
            nc.vector.tensor_copy(cols[:, :], psM[:, 0:NCOLS]).then_inc(cols_ready, 1)
            x_stats(2)
            x_stats(3)
            split_x(0)
            x_shift(slice(TPB, TILES), 2)
            dve.wait_ge(bias_in, 32)
            for b in range(BLOCKS):
                if b + 1 < BLOCKS:
                    scale_x(b + 1)
                for r in range(4 * b, 4 * b + 4):
                    if r % 4 == 2 and b + 1 < BLOCKS:
                        split_x(b + 1)
                    _, w, half = QK_ROUNDS[r]
                    c = (C_BQ, C_BK)[w] + half
                    dve.wait_ge(part0, r + 1)
                    if r >= 2:
                        dve.wait_ge(parts_ready, r - 1)
                    nc.vector.scalar_tensor_tensor(out=part_rest[:, r % 2, :], in0=psT[:, r % 4, :],
                                                   scalar=cols[:, c:c + 1], in1=parts[:, r % 3, 0, :],
                                                   op0=ALU.add, op1=ALU.subtract).then_inc(bank_read, 1)
                    dve.wait_ge(bank_read, r + 1)
                    nc.vector.tensor_copy(parts[:, r % 3, 1, :], part_rest[:, r % 2, :])\
                        .then_inc(rest_ready, 1)
                for v in range(2 * b, 2 * b + 2):
                    dve.wait_ge(v_proj, v + 1)
                    bank = (psA, psM)[v % 2]
                    nc.vector.tensor_tensor(out=V[:, 2 * v:2 * v + 2, :],
                                            in0=bank[:, :].rearrange("p (t n) -> p t n", t=2),
                                            in1=bv_all[:, :].unsqueeze(1).to_broadcast([P, 2, D]),
                                            op=ALU.add).then_inc(v_ready, 1)

            dve.wait_ge(consts_ready, 4)

            def reduce_bank(s):
                _, g, i, k = s
                _, heads, _, width, slot = max_jobs(i)[k]
                dve.wait_ge(s_filled, S_NO[s] + 1)
                nc.vector.tensor_reduce(pmax[:, (i // TPB) % 2, i % TPB, heads[0]:heads[-1] + 1, slot],
                                        psS[:, S_NO[s] % SRING, 0:len(heads) * width]
                                        .rearrange("p (h n) -> p h n", n=width),
                                        axis=AX.X, op=ALU.max).then_inc(s_read, 1)

            def block_max(g, b):
                n = g * BLOCKS + b
                dve.wait_ge(s_read, S_NO["max", g, b * TPB + TPB - 1, len(max_jobs(b * TPB + TPB - 1)) - 1] + 1)
                if n >= 2:
                    dve.wait_ge(mparts_ready, n - 1)
                nc.vector.tensor_reduce(negmax[:, b % 2, :].rearrange("p (h t) -> p t h", t=TPB),
                                        pmax[:, b % 2, :, :, 0:2 + b],
                                        axis=AX.X, op=ALU.max, negate=True).then_inc(rowmax_ready, 1)

            def max_rows(s):
                _, g, b = s
                n = g * BLOCKS + b
                dve.wait_ge(s_filled, S_NO[s] + 1)
                if n >= 2:
                    dve.wait_ge(mrows_in[b % 2], n // 2 * (16 * HG))
                nc.vector.tensor_copy(mrows[:, b % 2, :],
                                      psS[:, S_NO[s] % SRING, :].bitcast(bf16)[0:MROWS * HG * TPB, 0:P])\
                    .then_inc(mrows_ready, 1)
                dve.wait_ge(mrows_ready, n + 1)
                dve.sem_inc(s_read, 1)

            def normalise(s):
                _, g, b = s
                dve.wait_ge(s_filled, S_NO[s] + 1)
                v = psS[:, S_NO[s] % SRING, :].rearrange("p (t h n) -> p t h n", t=TPB, h=HG)
                nc.vector.reciprocal(recip[:, b % 2, :].rearrange("p (t h) -> p t h", t=TPB),
                                     v[:, :, :, DH]).then_inc(recip_ready, 1)
                dve.wait_ge(recip_ready, g * BLOCKS + b + 1)
                o = O[:, b * TPB:(b + 1) * TPB, g * HG * DH:(g + 1) * HG * DH]\
                    .rearrange("p t (h d) -> p t h d", d=DH)
                r = recip[:, b % 2, :].rearrange("p (t h) -> p t h", t=TPB)\
                    .unsqueeze(3).to_broadcast([P, TPB, HG, DH])
                nc.vector.tensor_tensor(out=o, in0=v[:, :, :, 0:DH], in1=r, op=ALU.mult).then_inc(s_read, 1)

            def lo_from_psum(s, hi_done, dst, hi, where):
                _, b, c = s
                dve.wait_ge(hi_done, b * DC + c + 1)
                nc.vector.tensor_tensor(out=dst[:, c, where], in0=psS[:, S_NO[s] % SRING, :],
                                        in1=hi[:, c, where].bitcast(f32), op=ALU.subtract).then_inc(s_read, 1)

            def residual(s):
                _, b, v = s
                if v == 0:
                    dve.wait_ge(xb_ready, b + 1)
                dve.wait_ge(s_filled, S_NO[s] + 1)
                t = b * TPB + 2 * v
                nc.vector.tensor_tensor(out=X1[:, t:t + 2, :],
                                        in0=psS[:, S_NO[s] % SRING, :].rearrange("p (t n) -> p t n", t=2),
                                        in1=X1[:, t:t + 2, :], op=ALU.add).then_inc(s_read, 1)
                dve.wait_ge(s_read, S_NO[s] + 1)
                for x in range(t, t + 2):
                    last = nc.vector.bn_stats(stats[:, x, :], X1[:, x, :])
                if v == 0:
                    return
                link(last)
                k = b * TPB
                for x in range(k, k + TPB):
                    last = nc.vector.bn_aggr(meanvar[:, x, :], stats[:, x, :])
                link(last)
                nc.vector.tensor_scalar(var_eps[:, k:k + TPB], meanvar[:, k:k + TPB, 1], EPS, None,
                                        ALU.add).then_inc(var2, 1)

            def norm2(b):
                k = b * TPB
                dve.wait_ge(rstd2, b + 1)
                link(nc.vector.scalar_tensor_tensor(out=lnshift[:, k:k + TPB], in0=meanvar[:, k:k + TPB, 0],
                                                    scalar=-1.0, in1=rstd[:, k:k + TPB],
                                                    op0=ALU.mult, op1=ALU.mult))
                if b >= 1:
                    dve.wait_ge(s_filled, S_NO["x2T", b - 1, DC - 1] + 1)
                for t in range(TPB):
                    last = nc.vector.tensor_scalar(xh2[:, t, :], X1[:, k + t, :],
                                                   rstd[:, k + t:k + t + 1], lnshift[:, k + t:k + t + 1],
                                                   ALU.mult, ALU.add)
                last.then_inc(xh2_ready, 1)

            for s in ORDER:
                if s[0] == "max":
                    reduce_bank(s)
                elif s[0] == "rowmax":
                    block_max(*s[1:])
                elif s[0] == "rowmaxT":
                    max_rows(s)
                elif s[0] == "norm":
                    normalise(s)
                    if s[1:] == (GROUPS - 1, 0):
                        dve.wait_ge(wsplit_hi, 1)
                        nc.vector.tensor_tensor(out=Wol[:, :, :], in0=wo_raw[:, :, :],
                                                in1=Woh[:, :, :].bitcast(f32),
                                                op=ALU.subtract).then_inc(wsplit, 1)
                elif s[0] == "oT":
                    lo_from_psum(s, oT_hi, OTl, OTh, slice(0, BW))
                elif s[0] == "oproj":
                    residual(s)
                elif s[0] == "xh2":
                    norm2(s[1])
                elif s[0] == "x2T":
                    lo_from_psum(s, x2_hi, X2l, X2h, slice(s[1] * BW, (s[1] + 1) * BW))

            n = 1
            for k in range(IC):
                n += 1
                dve.wait_ge(wsplit_hi, n)
                for c in range(DC):
                    last = nc.vector.tensor_tensor(out=ug_chunk(UGl, c, k), in0=ug_chunk(wug, c, k),
                                                   in1=ug_chunk(UGh, c, k).bitcast(f32), op=ALU.subtract)
                last.then_inc(wsplit, 1)
                if k == 1:
                    n += 1
                    dve.wait_ge(wsplit_hi, n)
                    nc.vector.tensor_tensor(out=Dl[:, :, :], in0=wd, in1=Dh[:, :, :].bitcast(f32),
                                            op=ALU.subtract).then_inc(wsplit, 1)

            with dve.Fori(0, BLOCKS) as b:
                for k in range(IC):
                    dve.wait_ge(silu_ready, b * IC + k + 1)
                    if k >= 2:
                        dve.wait_ge(h_hi, b * IC + k - 1 + START)
                    else:
                        dve.wait_ge(h_hi, b * IC + START)
                    nc.vector.scalar_tensor_tensor(out=hf[:, k % 2, :], in0=psT[:, 2 * (k % 2) + 1, :],
                                                   scalar=cols[:, C_WUG + k:C_WUG + k + 1],
                                                   in1=sg[:, k % 2, :], op0=ALU.mult,
                                                   op1=ALU.mult).then_inc(h_ready, 1)
                    dve.wait_ge(h_hi, b * IC + k + 1 + START)
                    nc.vector.tensor_tensor(out=Hl[:, k % 4, :], in0=hf[:, k % 2, :],
                                            in1=Hh[:, k % 4, :].bitcast(f32),
                                            op=ALU.subtract).then_inc(h_split, 1)
                dve.wait_ge(y_out, b * 16 + START)
                dve.wait_ge(down_k, b * IC + IC + START)
                for t in range(TPB):
                    nc.vector.tensor_tensor(out=yst[:, t, :], in0=down_bank(t),
                                            in1=X1[:, ds(b * TPB + t, 1), :].rearrange("p a n -> p (a n)"),
                                            op=ALU.add).then_inc(y_ready, 1)

        @block.tensor
        def _(pe):
            pe.sem_inc(down_k, START)
            pe.wait_ge(consts_ready, 2)

            def transpose_x(b):
                pe.wait_ge(xh_ready, TPB * (b + 1))
                for c in range(DC):
                    n = b * DC + c
                    if n >= 2:
                        pe.wait_ge(xnf_ready, n - 1)
                    for t in range(TPB):
                        last = nc.tensor.transpose(psS[:, n % 2, t * P:(t + 1) * P],
                                                   xin[:, b * TPB + t, c * P:(c + 1) * P], identf[:, :])
                    last.then_inc(xT, 1)

            def hilo(bank, lh, ll, rh, rl):
                n = len(lh)
                for c in range(n):
                    for m, (a, x) in enumerate(((lh[c], rh[c]), (lh[c], rl[c]), (ll[c], rh[c]))):
                        last = nc.tensor.matmul(bank, a, x, start=(c == 0 and m == 0),
                                                stop=(c == n - 1 and m == 2))
                return last

            transpose_x(0)
            pe.wait_ge(rows_in, 16 * 8)
            nc.tensor.transpose(psM[:, 0:NCOLS], rows[:, :], identf[0:NCOLS, 0:NCOLS]).then_inc(rowsT, 1)
            pe.wait_ge(wa_split, 1)
            for b in range(BLOCKS):
                pe.wait_ge(xsplit, DC * (b + 1))
                xh = [XTh[:, b % 2, c, :] for c in range(DC)]
                xl = [XTl[:, b % 2, c, :] for c in range(DC)]
                for r in range(4 * b, 4 * b + 4):
                    if r % 4 == 2 and b + 1 < BLOCKS:
                        transpose_x(b + 1)
                    _, w, half = QK_ROUNDS[r]
                    f = slice(half * P, (half + 1) * P)
                    if r >= 4:
                        pe.wait_ge(bank_read, r - 3)
                    hilo(psT[:, r % 4, :], [WAh[:, w, c, f] for c in range(DC)],
                         [WAl[:, w, c, f] for c in range(DC)], xh, xl).then_inc(qk_proj, 1)
                for v in range(2 * b, 2 * b + 2):
                    if v >= 2:
                        pe.wait_ge(v_ready, v - 1)
                    if v == 1:
                        pe.wait_ge(cols_ready, 1)
                    for t in range(2):
                        k = slice(((2 * v + t) % TPB) * P, ((2 * v + t) % TPB + 1) * P)
                        last = hilo((psA, psM)[v % 2][:, t * D:(t + 1) * D],
                                    [XTh[:, b % 2, c, k] for c in range(DC)],
                                    [XTl[:, b % 2, c, k] for c in range(DC)],
                                    [WAh[:, 2, c, :] for c in range(DC)],
                                    [WAl[:, 2, c, :] for c in range(DC)])
                    last.then_inc(v_proj, 1)

            def prep(n):
                q, bank = n % 4, psT[:, T_NO["prep", n] % TRING * EH, :]
                t_slot("prep", n)
                if n < 8:
                    if n == 0:
                        pe.wait_ge(wffn_in, 48)
                    c = n // 4
                    for t in range(4):
                        last = nc.tensor.transpose(bank[:, t * P:(t + 1) * P],
                                                   wug_raw[:, 4 * q + t, c * P:(c + 1) * P], identf[:, :])
                elif n < 16:
                    c = (n - 8) // 4
                    if n == 8:
                        pe.wait_ge(hadm_ready, 1)
                        pe.wait_ge(t_read, T_NO["prep", 7] + 1)
                    nc.tensor.matmul(bank, hadp[:, :], WT[:, 0, q * BW:(q + 1) * BW],
                                     start=True, stop=False)
                    last = nc.tensor.matmul(bank, (hadp, hadm)[c][:, :],
                                            WT[:, 1, q * BW:(q + 1) * BW], start=False, stop=True)
                elif n < 20:
                    if n == 16:
                        pe.wait_ge(wd_rot, 1)
                    for j in range(2):
                        for c in range(DC):
                            k = 2 * q + j
                            last = nc.tensor.transpose(bank[:, j * D + c * P:j * D + (c + 1) * P],
                                                       WDx[:, c, k * P:(k + 1) * P], identf[:, :])
                else:
                    pe.wait_ge(t_read, T_NO["prep", n - 4] + 1)
                    last = nc.tensor.matmul(bank, hadp[:, :],
                                            WDT[:, 2 * q:2 * q + 2, :].rearrange("p c o -> p (c o)"),
                                            start=True, stop=True)
                last.then_inc(t_filled, 1)

            def t_slot(*s):
                if T_NO[s] >= TRING:
                    pe.wait_ge(t_read, T_NO[s] - TRING + 1)

            def s_bank(s):
                if S_NO[s] >= SRING:
                    pe.wait_ge(s_read, S_NO[s] - SRING + 1)
                return psS[:, S_NO[s] % SRING, :]

            def max_scores(s):
                _, g, i, k = s
                kind, heads, k0, width, _ = max_jobs(i)[k]
                if g == 0 and k == 0 and i % TPB == 0:
                    pe.wait_ge(ops0_in[i // TPB], 16 * 2 * SLOTS)
                elif i == 0 and k == 0:
                    pe.wait_ge(ops_in, g * (16 * 2 * SLOTS))
                bank = s_bank(s)
                if kind == "diag":
                    nc.tensor.matmul(bank, identb[:, :], mask[:, :, :], start=True, stop=False)
                for m, h in enumerate(heads):
                    last = nc.tensor.matmul(bank[:, m * width:(m + 1) * width],
                                            QA[0:ROWS, g % 2, h, i * P:(i + 1) * P],
                                            KA[0:ROWS, g % 2, h, k0:k0 + width],
                                            start=(kind != "diag"),
                                            stop=(kind != "diag" or m == len(heads) - 1))
                last.then_inc(s_filled, 1)

            def exp_scores(s):
                _, g, b, j, h = s
                off = max(j - TPB * b, 0) * P
                t_slot(*s)
                if j == 0 and h == 0:
                    pe.wait_ge(mrows_in[b % 2], ((g * BLOCKS + b) // 2 + 1) * (16 * HG))
                for m in range(EH):
                    last = nc.tensor.matmul(
                        psT[:, T_NO[s] % TRING * EH + m, off:BW],
                        KA[0:ROWS + MROWS, g % 2, h + m, j * P:(j + 1) * P],
                        QA[0:ROWS + MROWS, g % 2, h + m, b * BW + off:(b + 1) * BW],
                        start=True, stop=True)
                last.then_inc(t_filled, 1)

            def product_v(g, b, j):
                off = max(j - TPB * b, 0) * P
                if is_diag(b, j):
                    pe.wait_ge(masked, diag_no(g, b, j))
                else:
                    pe.wait_ge(t_read, t_done(g, b, j))
                if j == 0 and g + b:
                    pe.wait_ge(av_out, g * BLOCKS + b)
                if j == TPB * b:
                    pe.wait_ge(vg_ready, g * BLOCKS + b + 1)
                for h in range(HG):
                    last = nc.tensor.matmul(psA[32 * h:32 * h + 32, off:BW], VG[:, j, h, :],
                                            PR[:, unit_no(g, b, j) % PRING, h, off:BW],
                                            start=(j == 0), stop=(j == TPB * (b + 1) - 1))
                last.then_inc(av_done, 1)

            def transposes(s, rows_of, c):
                bank = s_bank(s)
                for t in range(TPB):
                    last = nc.tensor.transpose(bank[:, t * P:(t + 1) * P],
                                               rows_of(t)[:, c * P:(c + 1) * P], identf[:, :])
                last.then_inc(s_filled, 1)

            pe.wait_ge(consts_ready, 4)
            pe.wait_ge(v_ready, TILES // 2)
            pe.wait_ge(bank_read, len(QK_ROUNDS))
            first_exp = True
            for s in ORDER:
                if s[0] == "max":
                    max_scores(s)
                elif s[0] == "rowmaxT":
                    _, g, b = s
                    pe.wait_ge(mparts_ready, g * BLOCKS + b + 1)
                    nc.tensor.transpose(s_bank(s).bitcast(bf16)[0:MROWS * HG * TPB, 0:P],
                                        mparts[:, b % 2, :, :, :].rearrange("p h m t -> p (h m t)"),
                                        identb[:, :]).then_inc(s_filled, 1)
                elif s[0] == "prep":
                    prep(s[1])
                elif s[0] == "exp":
                    if first_exp:
                        pe.wait_ge(ones_in, 16 * 2 * HG)
                        first_exp = False
                    exp_scores(s)
                elif s[0] == "av":
                    product_v(*s[1:])
                elif s[0] == "norm":
                    _, g, b = s
                    bank = s_bank(s)
                    pe.wait_ge(av_out, g * BLOCKS + b + 1)
                    for t in range(TPB):
                        last = nc.tensor.transpose(bank[:, t * P:(t + 1) * P],
                                                   avT[:, b % 2, t * P:(t + 1) * P], identf[:, :])
                    last.then_inc(s_filled, 1)
                elif s[0] == "oT":
                    _, b, c = s
                    pe.wait_ge(s_read, S_NO["norm", GROUPS - 1, b] + 1)
                    transposes(s, lambda t: O[:, b * TPB + t, :], c)
                elif s[0] == "oproj":
                    _, b, v = s
                    pe.wait_ge(s_read, S_NO["oT", b, DC - 1] + 1)
                    pe.wait_ge(wsplit, 1)
                    bank = s_bank(s)
                    for t in range(2):
                        k = slice((2 * v + t) * P, (2 * v + t + 1) * P)
                        last = hilo(bank[:, t * D:(t + 1) * D],
                                    [OTh[:, c, k] for c in range(DC)], [OTl[:, c, k] for c in range(DC)],
                                    [Woh[:, c, :] for c in range(DC)], [Wol[:, c, :] for c in range(DC)])
                    last.then_inc(s_filled, 1)
                elif s[0] == "x2T":
                    pe.wait_ge(xh2_ready, s[1] + 1)
                    transposes(s, lambda t: xh2[:, t, :], s[2])
            pe.wait_ge(s_read, len(S_STEPS))
            pe.wait_ge(t_read, len(T_STEPS))

            with pe.Fori(0, BLOCKS) as b:
                def down(k):
                    pe.wait_ge(h_split, b * IC + k + 1)
                    for t in range(TPB):
                        if k == 0:
                            pe.wait_ge(y_ready, b * TPB + START)
                        sl = slice(t * P, (t + 1) * P)
                        for m, (a, x) in enumerate(((Hh, Dh), (Hh, Dl), (Hl, Dh))):
                            last = nc.tensor.matmul(down_bank(t), a[:, k % 4, sl], x[:, k, :],
                                                    start=(k == 0 and m == 0),
                                                    stop=(k == IC - 1 and m == 2))
                    last.then_inc(down_k, 1)

                for k in range(IC):
                    pe.wait_ge(wsplit, k + 2 + (k >= 2))
                    if k >= 2:
                        pe.wait_ge(h_ready, b * IC + k - 1 + START)
                    else:
                        pe.wait_ge(h_ready, b * IC + START)
                    for which in range(2):
                        f = slice((1 - which) * INTER + k * P, (1 - which) * INTER + (k + 1) * P)
                        xs = ds(b * BW, BW)
                        last = hilo(psT[:, 2 * (k % 2) + which, :],
                                    [UGh[:, c, f] for c in range(DC)], [UGl[:, c, f] for c in range(DC)],
                                    [X2h[:, c, xs] for c in range(DC)], [X2l[:, c, xs] for c in range(DC)])
                    last.then_inc(ug_mm, 1)
                    if k >= 2:
                        down(k - 2)
                down(IC - 2)
                down(IC - 1)


_INS = ["L0_attn_X", "L0_attn_ln_g", "L0_attn_ln_b", "L0_attn_Wq", "L0_attn_bq", "L0_attn_Wk",
        "L0_attn_bk", "L0_attn_Wv", "L0_attn_bv", "L0_attn_Wo", "L0_attn_bo", "L0_ffn_SU_ug",
        "L0_ffn_SU_dp", "L0_ffn_Wscale_ug", "L0_ffn_Wscale_dp", "L0_ffn_W_up", "L0_ffn_W_gate",
        "L0_ffn_W_down"]


def kernel(**inputs):
    import numpy as np
    import concourse.bacc as bacc
    from concourse.bass_utils import run_bass_kernel_spmd

    nc = bacc.Bacc("TRN2", target_bir_lowering=False, num_devices=1)
    arrays, args = {}, []
    for name in _INS:
        a = np.ascontiguousarray(inputs[name])
        arrays[name] = a
        args.append(nc.dram_tensor(name, a.shape, mybir.dt.from_np(a.dtype), kind="ExternalInput").ap())
    had = np.ones((1, 1), np.float32)
    while had.shape[0] < P:
        had = np.block([[had, had], [had, -had]])
    arrays["had"] = np.ascontiguousarray(had, np.float32)
    args.append(nc.dram_tensor("had", (P, P), mybir.dt.float32, kind="ExternalInput").ap())
    args.append(nc.dram_tensor("out", (1, SEQ, D), mybir.dt.float32, kind="ExternalOutput").ap())
    build(nc, *args)
    r = run_bass_kernel_spmd(nc, [arrays], core_ids=[0])
    return r.results[0]["out"]
```

```python
import concourse.bass as bass
from concourse import mybir
from contextlib import ExitStack

SEQ, D, HEADS, INTER = 2048, 256, 16, 1024
P = 128
DH = D // HEADS
TILES = SEQ // P
BW = 512
BLOCKS = SEQ // BW
TPB = BW // P
DC = D // P
IC = INTER // P
HG = 4
GROUPS = HEADS // HG
EPS = 1e-5
START = 1
NEG = -1.0e30
LOWEST = -3.0e38
Q_SLOTS = (0, 0, 0, 1, 1, 2)
K_SLOTS = (0, 1, 2, 0, 1, 0)
SLOTS = len(Q_SLOTS)
ROWS = SLOTS * DH
MROWS = 3
NSLOT = 2 + BLOCKS - 1
PRING = 4
C_G, C_B, C_BQ, C_BK, C_SUG, C_SDP, C_WUG, C_WDP = 0, 2, 4, 6, 8, 10, 18, 34
NCOLS = 36

EH = 2
SRING = 3
TRING = 4 // EH
PARTS, RESTS = 6, 4
PREP_ROUNDS = 24


def max_jobs(i):
    full, rem = divmod(i, TPB)
    jobs = [("diag", (0, 1, 2, 3), i * P, P, 0)]
    per = BW // (rem * P) if rem else 0
    for h in range(0, HG, per) if rem else ():
        jobs.append(("part", tuple(range(h, h + per)), full * BW, rem * P, 1))
    for f in range(full):
        for h in range(HG):
            jobs.append(("part", (h,), f * BW, BW, 2 + f))
    return jobs


UNITS = sum(TPB * (b + 1) for b in range(BLOCKS))


def unit_no(g, b, j):
    return g * UNITS + sum(TPB * (x + 1) for x in range(b)) + j


def is_diag(b, j):
    return j >= TPB * b


def plan():
    TO_READER, TO_PE, ROWS_DMA = 0.18, 0.10, 4.0
    t = dve = act = 0.0
    steps = []
    maxq = []
    for g in range(GROUPS):
        for i in range(TILES):
            maxq += [("max", g, i, k) for k in range(len(max_jobs(i)))]
            if i % TPB == TPB - 1:
                maxq.append(("rowmax", g, i // TPB))
    units = [(g, b, j) for g in range(GROUPS) for b in range(BLOCKS) for j in range(TPB * (b + 1))]
    expq = [u + (h,) for u in units for h in range(0, HG, EH)]
    avq = list(units)
    prepq = list(range(PREP_ROUNDS))
    s_read, t_read, av_at = [], [], {}
    rows_at, exp_at, later = {}, {}, []
    ops_at = {0: 0.0, 1: 30.0}
    psA_free, chain_block = 0.0, 0

    def s_free():
        return s_read[-SRING] if len(s_read) >= SRING else 0.0

    def t_free():
        return t_read[-TRING] if len(t_read) >= TRING else 0.0

    while maxq or expq or avq or later or prepq:
        cand = []
        for n, (r, st) in enumerate(later):
            if st[0] == "oT" and st[1] != chain_block:
                continue
            cand.append((r if st[0] == "xh2" else max(r, s_free()), 0, "later", n))
        if maxq and maxq[0][1] in ops_at:
            cand.append((max(s_free(), ops_at[maxq[0][1]]), 1, "max", 0))
        if avq and avq[0] in exp_at:
            g, b, j = avq[0]
            cand.append((max(exp_at[avq[0]], psA_free if j == 0 else 0.0), 2, "av", 0))
        if expq:
            g, b, j, h = expq[0]
            u = unit_no(g, b, j)
            if (g, b) in rows_at and (u < PRING or u - PRING in av_at) and not (g == GROUPS - 1 and prepq):
                cand.append((max(t_free(), rows_at[g, b], av_at.get(u - PRING, 0.0)), 1.5, "exp", 0))
        if prepq:
            if prepq[0] < 16 or expq[0] > (0, 3, 0, 0):
                cand.append((t_free(), 4, "prep", 0))
        now = [c for c in cand if c[0] <= t]
        r, _, kind, n = min(now, key=lambda c: c[1]) if now else min(cand)
        t = max(t, r)
        if kind == "max":
            st = maxq.pop(0)
            steps.append(st)
            what, heads, _, width, _ = max_jobs(st[2])[st[3]]
            cols = len(heads) * width
            t += cols * (2 if what == "diag" else 1) / 2400
            dve = max(dve, t + TO_READER) + cols / 960 + 0.07
            s_read.append(dve + TO_PE)
            if maxq and maxq[0][0] == "rowmax":
                st = maxq.pop(0)
                steps.append(st)
                dve += 0.4
                later.append((dve + 3.0, ("rowmaxT",) + st[1:]))
        elif kind == "exp":
            g, b, j, h = expq.pop(0)
            w = BW - max(j - TPB * b, 0) * P
            t += EH * w / 2400
            steps.append(("exp", g, b, j, h))
            act = max(act, t + TO_READER) + EH * w / 1200 + 0.06
            t_read.append(act + TO_PE)
            if h + EH == HG:
                exp_at[g, b, j] = act + TO_PE + (1.5 if is_diag(b, j) else 0.0)
        elif kind == "av":
            g, b, j = avq.pop(0)
            w = BW - max(j - TPB * b, 0) * P
            t += 4 * w / 2400 + 0.08
            steps.append(("av", g, b, j))
            av_at[unit_no(g, b, j)] = t + 0.1
            if j == TPB * (b + 1) - 1:
                steps.append(("avout", g, b))
                act = max(act, t + TO_READER) + 0.5
                psA_free = act + TO_PE
                later.append((psA_free, ("norm", g, b)))
                if b == BLOCKS - 1:
                    ops_at[g + 2] = t + 12.0
        elif kind == "prep":
            n = prepq.pop(0)
            steps.append(("prep", n))
            t += 0.25 if n < 8 or 16 <= n < 20 else 1.7
            act = max(act, t + TO_READER) + 0.5
            t_read.append(act + TO_PE)
        else:
            st = later.pop(n)[1]
            b = st[-1]
            if st[0] == "xh2":
                steps.append(st)
                dve += 1.6
                later.append((dve + 0.2, ("x2T", b)))
            elif st[0] in ("rowmaxT", "norm"):
                steps.append(st)
                t += 0.06 if st[0] == "rowmaxT" else 0.22
                dve = max(dve, t + TO_READER) + (0.3 if st[0] == "rowmaxT" else 0.8)
                s_read.append(dve + TO_PE)
                if st[0] == "rowmaxT":
                    rows_at[st[1:]] = dve + ROWS_DMA
                elif st[1] == GROUPS - 1:
                    later.append((dve + 0.2, ("oT", b)))
            else:
                for c in range(2):
                    steps.append((st[0], b, c))
                    t = max(t, s_free()) + (1.3 if st[0] == "oproj" else 0.25)
                    dve = max(dve, t + TO_READER + (0.0 if st[0] == "oproj" else 0.6)) + 0.6
                    s_read.append(dve + TO_PE)
                if st[0] == "oT":
                    later.append((dve + 0.2, ("oproj", b)))
                elif st[0] == "oproj":
                    dve += 2.0
                    later.append((dve + 4.0, ("xh2", b)))
                else:
                    chain_block += 1
    return steps


ORDER = plan()
LAST = BLOCKS - 1
TAIL = [("wsplit", 0), ("wsplit", 1), ("norm", GROUPS - 1, LAST), ("ug", 0), ("wsplit", 2),
        ("wsplit", "down"), ("oT", LAST, 0), ("oT", LAST, 1), ("ug", 1), ("wsplit", 3), ("ug", 2),
        ("wsplit", 4), ("down", 0), ("oproj", LAST, 0), ("oproj", LAST, 1), ("ug", 3), ("wsplit", 5),
        ("down", 1), ("wsplit", 6), ("xh2", LAST), ("ug", 4), ("down", 2), ("wsplit", 7),
        ("ug", 5), ("down", 3), ("x2T", LAST, 0), ("x2T", LAST, 1), ("ug", 6), ("down", 4),
        ("ug", 7), ("down", 5)]
chain = [s for s in TAIL if s[0] not in ("wsplit", "ug", "down")]
assert ORDER[-len(chain):] == chain
ORDER[-len(chain):] = TAIL
W_NO = {s[1]: n + 1 for n, s in enumerate(s for s in TAIL if s[0] == "wsplit")}
S_STEPS = [s for s in ORDER if s[0] in ("max", "rowmaxT", "norm", "oT", "oproj", "x2T")]
T_STEPS = [s for s in ORDER if s[0] in ("exp", "prep")]
S_NO = {s: n for n, s in enumerate(S_STEPS)}
T_NO = {s: n for n, s in enumerate(T_STEPS)}
S_BANK = [n % SRING if s not in TAIL else n % 2 for n, s in enumerate(S_STEPS)]
S_PREV = [max([m for m in range(n) if S_BANK[m] == S_BANK[n]], default=None) for n in range(len(S_STEPS))]


def t_done(g, b, j):
    return T_NO["exp", g, b, j, HG - EH] + 1


def diag_no(g, b, j):
    return g * TILES + j + 1


def build(nc, X, ln_g, ln_b, Wq, bq, Wk, bk, Wv, bv, Wo, bo, SU_ug, SU_dp, Ws_ug, Ws_dp,
          W_up, W_gate, W_down, had, out):
    f32, bf16, f32r = mybir.dt.float32, mybir.dt.bfloat16, mybir.dt.float32r
    ALU = mybir.AluOpType
    ACT = mybir.ActivationFunctionType
    AX = mybir.AxisListType
    ds = bass.ds

    nc.disable_value_cache = True
    ctx = ExitStack()
    with ctx:
        sem_of = {}

        def sem(name):
            sem_of[name] = ctx.enter_context(nc.semaphore(name))
            return sem_of[name]

        size = {f32: 4, f32r: 4, bf16: 2}
        top = [(nc.sbuf_base + 63) // 64 * 64]

        def area(nbytes):
            at = top[0]
            top[0] += (nbytes + 63) // 64 * 64
            return at

        def put(name, shape, dt, at=None):
            n = size[dt]
            for s in shape[1:]:
                n *= s
            if at is None:
                at = area(n)
            return nc.alloc_sbuf_tensor_at(name, shape, dt, offset=at), at + n

        def sb(name, shape, dt):
            return put(name, shape, dt)[0]

        identf = sb("identf", [P, P], f32)
        identb = sb("identb", [P, P], bf16)
        zerob = sb("zerob", [P, P], bf16)
        mask = sb("mask", [P, HG, P], bf16)
        hadp = sb("hadp", [P, P], f32)
        hadm = sb("hadm", [P, P], f32)
        rows = sb("rows", [NCOLS, P], f32)
        cols = sb("cols", [P, NCOLS], f32)
        bv_all = sb("bv_all", [P, D], f32)
        bo_all = sb("bo_all", [P, D], f32)
        stats = sb("stats", [P, TILES, 6], f32)
        meanvar = sb("meanvar", [P, TILES, 2], f32)
        halves = sb("halves", [P, TILES], f32)
        var_eps = sb("var_eps", [P, TILES], f32)
        rstd = sb("rstd", [P, TILES], f32)
        lnshift = sb("lnshift", [P, TILES], f32)
        pmax = sb("pmax", [P, 2, TPB, HG, NSLOT], f32)
        negmax = sb("negmax", [P, 2, TPB * HG], f32)
        mrest = sb("mrest", [P, 2, TPB * HG], f32)
        mparts = sb("mparts", [P, 2, HG, MROWS, TPB], bf16)
        mrows = sb("mrows", [MROWS * HG * TPB, 2, P], bf16)
        recip = sb("recip", [P, 2, TPB * HG], f32)

        a_ops = area(2 * 2 * HG * SEQ * 2)
        QA, _ = put("QA", [P, 2, HG, SEQ], bf16, a_ops)
        KA, _ = put("KA", [P, 2, HG, SEQ], bf16, a_ops + 2 * HG * SEQ * 2)
        a_v = area(TILES * D * 4)
        V, _ = put("V", [P, TILES, D], f32, a_v)
        a_vg = area(TILES * HG * 32 * 4)
        VG, _ = put("VG", [P, TILES, HG, 32], f32, a_vg)
        a_pr = area(PRING * HG * BW * 4)
        PR, _ = put("PR", [P, PRING, HG, BW], f32, a_pr)
        avT = sb("avT", [P, 2, BW], f32)
        a_o = area(TILES * D * 4)
        xin, _ = put("xin", [P, TILES, D], f32, a_o)
        O, _ = put("O", [P, TILES, D], f32, a_o)
        WUG = sb("WUG", [P, 2 * IC * D], f32)
        WD = sb("WD", [P, IC * D], f32)
        a_e = area(32 * 1024)
        assert top[0] <= nc.sbuf_usable_end, (top[0], nc.sbuf_usable_end)

        XTh, n = put("XTh", [P, 2, DC, BW], f32r, a_e)
        XTl, n = put("XTl", [P, 2, DC, BW], f32r, n)
        xnf, n = put("xnf", [P, 2, BW], f32, n)
        WAh, n = put("WAh", [P, 3, DC, D], f32r, n)
        WAl, n = put("WAl", [P, 3, DC, D], f32r, n)
        wa_raw, _ = put("wa_raw", [P, 3, DC, D], f32, a_vg)
        WT, n = put("WT", [P, DC, 2 * INTER], f32, a_e)
        WDx, n = put("WDx", [P, DC, INTER], f32, n)
        WDT, n = put("WDT", [P, IC, D], f32, n)
        assert n <= a_e + 32 * 1024
        ones, n = put("ones", [MROWS, SEQ], bf16, a_pr)
        parts, n = put("parts", [P, PARTS, 3, BW], bf16, n)
        part_rest, n = put("part_rest", [P, RESTS, BW], f32, n)
        assert n <= a_pr + PRING * HG * BW * 4
        wug_raw = WUG[:, :].rearrange("p (t f) -> p t f", f=D)
        wug = WUG[:, :].rearrange("p (c o) -> p c o", c=DC)
        wd_raw = WD[:, :].rearrange("p (c i) -> p c i", c=DC)
        wd = WD[:, :].rearrange("p (c o) -> p c o", c=IC)

        quarter = HG * SEQ * 2
        X1, _ = put("X1", [P, TILES, D], f32, a_ops)
        Dh, n = put("Dh", [P, IC, D], f32r, a_ops + quarter)
        Dl, _ = put("Dl", [P, IC, D], f32r, n)
        X2h, _ = put("X2h", [P, DC, SEQ], f32r, a_ops + 2 * quarter)
        Hh, n = put("Hh", [P, 4, BW], f32r, a_ops + 3 * quarter)
        Hl, _ = put("Hl", [P, 4, BW], f32r, n)
        X2l, _ = put("X2l", [P, DC, SEQ], f32r, a_v)
        UGh, n = put("UGh", [P, DC, 2 * INTER], f32r, a_pr)
        UGl, _ = put("UGl", [P, DC, 2 * INTER], f32r, n)
        wo_raw, n = put("wo_raw", [P, DC, D], f32, a_e)
        Woh, n = put("Woh", [P, DC, D], f32r, n)
        Wol, n = put("Wol", [P, DC, D], f32r, n)
        OTh, n = put("OTh", [P, DC, BW], f32r, n)
        OTl, n = put("OTl", [P, DC, BW], f32r, n)
        xh2, n = put("xh2", [P, TPB, D], f32, n)
        sg, n = put("sg", [P, 2, BW], f32, n)
        hf, n = put("hf", [P, 2, BW], f32, n)
        yst, n = put("yst", [P, TPB, D], f32, n)
        assert n <= a_e + 32 * 1024

        psS = ctx.enter_context(nc.psum_tensor("psS", [P, SRING, BW], f32))
        psT = ctx.enter_context(nc.psum_tensor("psT", [P, 4, BW], f32))
        psA = ctx.enter_context(nc.psum_tensor("psA", [P, BW], f32))
        psM = psS[:, SRING - 1, :]

        scr = nc.dram_tensor("scr", (2, 3, D, SEQ), bf16, kind="Internal").ap()

        x_in = [sem(f"x_in{b}") for b in range(BLOCKS)]
        rows_in, wa_in, bias_in, had_in, wffn_in = (sem(n) for n in
            ("rows_in", "wa_in", "bias_in", "had_in", "wffn_in"))
        dve_link, pool_link = sem("dve_link"), sem("pool_link")
        consts_ready = sem("consts_ready")
        hadm_ready = sem("hadm_ready")
        rowsT, cols_ready = sem("rowsT"), sem("cols_ready")
        var_ready, rstd_ready, xh_ready = sem("var_ready"), sem("rstd_ready"), sem("xh_ready")
        xT, xnf_ready, xsplit = sem("xT"), sem("xnf_ready"), sem("xsplit")
        wa_split = sem("wa_split")
        qk_proj, part0, bank_read, rest_ready, parts_ready = (sem(n) for n in
            ("qk_proj", "part0", "bank_read", "rest_ready", "parts_ready"))
        scr_out = [sem(f"scr_out{i}") for i in range(PARTS)]
        v_proj, v_ready = sem("v_proj"), sem("v_ready")
        ops0_in = [sem(f"ops0_in{b}") for b in range(BLOCKS)]
        ops_in, ones_ready, ones_in = sem("ops_in"), sem("ones_ready"), sem("ones_in")
        wa_hi = sem("wa_hi")
        wd_rot = sem("wd_rot")
        vg_ready = sem("vg_ready")
        s_filled, s_read, t_filled, t_read = (sem(n) for n in ("s_filled", "s_read", "t_filled", "t_read"))
        rowmax_ready, mparts_ready, mrows_ready = (sem(n) for n in
            ("rowmax_ready", "mparts_ready", "mrows_ready"))
        mrows_in = [sem(f"mrows_in{i}") for i in range(2)]
        masked, av_done, av_out, recip_ready = (sem(n) for n in
            ("masked", "av_done", "av_out", "recip_ready"))
        xre_in, wo_in, xb_ready, wsplit_hi, wsplit = (sem(n) for n in
            ("xre_in", "wo_in", "xb_ready", "wsplit_hi", "wsplit"))
        oT_hi, var2, rstd2, xh2_ready, x2_hi = (sem(n) for n in
            ("oT_hi", "var2", "rstd2", "xh2_ready", "x2_hi"))
        ug_mm, silu_ready, h_ready, h_hi, h_split, down_k, y_ready, y_out = (sem(n) for n in
            ("ug_mm", "silu_ready", "h_ready", "h_hi", "h_split", "down_k", "y_ready", "y_out"))

        block = ctx.enter_context(nc.Block())

        QK_ROUNDS = [(b, w, half) for b in range(BLOCKS) for w in range(2) for half in range(DC)]

        def down_bank(t):
            return (psA, psM)[t // 2][:, t % 2 * D:(t % 2 + 1) * D]

        def at_start(b, k, n):
            return isinstance(b, int) and b * IC + k < n

        def ug_chunk(w, c, k):
            return w[:, c, :].rearrange("p (g k o) -> p g k o", g=2, o=P)[:, :, k, :]

        @block.sync
        def _(sp):
            sp.sem_inc(y_out, START)
            x_t = X.rearrange("a (t p) f -> p (a t) f", p=P)

            def load_x(b):
                sp.dma_start(xin[:, b * TPB:(b + 1) * TPB, :],
                             x_t[:, b * TPB:(b + 1) * TPB, :]).then_inc(x_in[b], 16)

            load_x(0)
            for w, src in enumerate((Wq, Wk, Wv)):
                sp.dma_start(wa_raw[:, w, :, :], src.rearrange("(c p) n -> p c n", p=P)).then_inc(wa_in, 16)
            load_x(1)
            for c, v in ((C_G, ln_g), (C_B, ln_b), (C_BQ, bq), (C_BK, bk), (C_SUG, SU_ug),
                         (C_SDP, SU_dp), (C_WUG, Ws_ug), (C_WDP, Ws_dp)):
                v = v.rearrange("(c p) -> c p", p=P)
                sp.dma_start(rows[c:c + v.shape[0], :], v).then_inc(rows_in, 16)
            load_x(2)
            load_x(3)
            for dst, src in ((bv_all, bv), (bo_all, bo)):
                sp.dma_start(dst[:, :], src.rearrange("(a n) -> a n", a=1).to_broadcast([P, D]))\
                  .then_inc(bias_in, 16)
            sp.dma_start(hadp[:, :], had).then_inc(had_in, 16)
            sp.wait_ge(ones_ready, 1)
            for par in range(2):
                for h in range(HG):
                    sp.dma_start(KA[ROWS:ROWS + MROWS, par, h, :], ones[:, :]).then_inc(ones_in, 16)
            for n, src in enumerate((W_up, W_gate)):
                sp.dma_start(wug_raw[:, n * IC:(n + 1) * IC, :],
                             src.rearrange("(t o) f -> o t f", o=P)).then_inc(wffn_in, 16)
            sp.dma_start(wd_raw, W_down.rearrange("(c o) i -> o c i", o=P)).then_inc(wffn_in, 16)

            def load_ops(g, toks, signal, slots=range(SLOTS)):
                for i in slots:
                    for w, dst, part in ((0, QA, Q_SLOTS[i]), (1, KA, K_SLOTS[i])):
                        src = scr[w, part, g * HG * DH:(g + 1) * HG * DH, toks].rearrange("(h d) n -> d h n", d=DH)
                        sp.dma_start(dst[i * DH:(i + 1) * DH, g % 2, :, toks], src).then_inc(signal, 16)

            def load_block(b, slots):
                if slots[0] == 0:
                    for i in range(PARTS):
                        if i < 4 * b + 4:
                            sp.wait_ge(scr_out[i], 16 * len(QK_ROUNDS[:4 * b + 4][i::PARTS]))
                load_ops(0, slice(b * BW, (b + 1) * BW), ops0_in[b], slots)

            for b in range(BLOCKS):
                for r in range(4 * b, 4 * b + 4):
                    _, w, half = QK_ROUNDS[r]
                    sp.wait_ge(parts_ready, r + 1)
                    sp.dma_start(scr[w, :, half * P:(half + 1) * P, b * BW:(b + 1) * BW]
                                 .rearrange("s f n -> f s n"), parts[:, r % PARTS, :, :]).then_inc(scr_out[r % PARTS], 16)
                    if b and r % 4:
                        load_block(b - 1, range(r % 4 * 2 - 2, r % 4 * 2))
            load_block(BLOCKS - 1, range(SLOTS))

            for s in ORDER:
                if s[0] == "rowmaxT":
                    _, g, b = s
                    sp.wait_ge(mrows_ready, g * BLOCKS + b + 1)
                    for h in range(HG):
                        dst = QA[ROWS:ROWS + MROWS, g % 2, h, b * BW:(b + 1) * BW]\
                            .rearrange("m (t q) -> m t q", t=TPB)
                        sp.dma_start(dst, mrows[h * MROWS * TPB:(h + 1) * MROWS * TPB, b % 2, :])\
                          .then_inc(mrows_in[b % 2], 16)
                    if (g, b) == (0, 1):
                        load_ops(1, slice(0, SEQ), ops_in)
                elif s[0] == "avout" and s[2] == BLOCKS - 1:
                    g = s[1]
                    sp.wait_ge(av_done, (g + 1) * UNITS)
                    if g + 2 < GROUPS:
                        sp.wait_ge(ops_in, (g + 1) * (16 * 2 * SLOTS))
                        load_ops(g + 2, slice(0, SEQ), ops_in)
                    elif g == GROUPS - 2:
                        sp.dma_start(X1[:, :, :], x_t).then_inc(xre_in, 16)
                        sp.wait_ge(t_read, T_NO["prep", PREP_ROUNDS - 1] + 1)
                        sp.dma_start(wo_raw[:, :, :], Wo.rearrange("(c p) n -> p c n", p=P)).then_inc(wo_in, 16)

            out_t = out.rearrange("a (t p) f -> p (a t) f", p=P)
            with sp.Fori(0, BLOCKS) as b:
                sp.wait_ge(y_ready, b * 2 + 2 + START)
                sp.dma_start(out_t[:, ds(b * TPB, TPB), :], yst[:, :, :]).then_inc(y_out, 16)
            sp.wait_ge(y_out, 16 * BLOCKS + START)

        @block.gpsimd
        def _(pool):
            chain = [0]

            def link(ins):
                chain[0] += 1
                ins.then_inc(pool_link, 1)
                pool.wait_ge(pool_link, chain[0])

            nc.gpsimd.memset(halves[:, :], -0.5).then_inc(consts_ready, 1)
            nc.gpsimd.memset(identf[:, :], 0.0)
            nc.gpsimd.memset(identb[:, :], 0.0)
            nc.gpsimd.memset(zerob[:, :], 0.0).then_inc(consts_ready, 1)
            link(nc.gpsimd.memset(mask[:, :, :], 0.0))
            nc.gpsimd.affine_select(out=identf[:, :], in_=identf[:, :], compare_op=ALU.not_equal, fill=1.0,
                                    base=0, pattern=[[-1, P]], channel_multiplier=1).then_inc(consts_ready, 1)
            nc.gpsimd.affine_select(out=identb[:, :], in_=identb[:, :], compare_op=ALU.not_equal, fill=1.0,
                                    base=0, pattern=[[-1, P]], channel_multiplier=1).then_inc(consts_ready, 1)
            nc.gpsimd.affine_select(out=mask[:, :, :], in_=mask[:, :, :], compare_op=ALU.is_ge, fill=NEG,
                                    base=0, pattern=[[0, HG], [-1, P]], channel_multiplier=1)\
                .then_inc(consts_ready, 1)
            nc.gpsimd.memset(pmax[:, :, :, :, :], LOWEST).then_inc(consts_ready, 1)

            pool.wait_ge(consts_ready, 6)
            nc.gpsimd.memset(ones[:, :], 1.0).then_inc(ones_ready, 1)
            pool.wait_ge(ones_ready, 1)

            def x_rstd(b):
                ts = slice(b * TPB, (b + 1) * TPB)
                pool.wait_ge(var_ready, b + 1)
                nc.gpsimd.tensor_tensor(out=rstd[:, ts], in0=var_eps[:, ts], in1=halves[:, ts],
                                        op=ALU.pow).then_inc(rstd_ready, 1)

            x_rstd(0)
            x_rstd(1)
            pool.wait_ge(wa_split, 1)
            link(nc.gpsimd.memset(VG[:, :, :, :], 1.0))
            pool.wait_ge(had_in, 16)
            nc.gpsimd.tensor_scalar(hadm[:, :], hadp[:, :], -1.0, None, ALU.mult).then_inc(hadm_ready, 1)

            for r in range(len(QK_ROUNDS)):
                if r % 4 == 0 and r < 8:
                    x_rstd(2 + r // 4)
                pool.wait_ge(rest_ready, r + 1)
                nc.gpsimd.tensor_tensor(out=parts[:, r % PARTS, 2, :], in0=part_rest[:, r % RESTS, :],
                                        in1=parts[:, r % PARTS, 1, :], op=ALU.subtract).then_inc(parts_ready, 1)

            def load_vg(g, c):
                src = V[:, c * TPB:(c + 1) * TPB, g * HG * DH:(g + 1) * HG * DH]\
                    .rearrange("p t (h d) -> p t h d", d=DH)
                nc.gpsimd.tensor_copy(VG[:, c * TPB:(c + 1) * TPB, :, 0:DH], src).then_inc(vg_ready, 1)

            for c in range(BLOCKS):
                pool.wait_ge(v_ready, 2 * (c + 1))
                load_vg(0, c)

            def split_max(g, b):
                n = g * BLOCKS + b
                pool.wait_ge(rowmax_ready, n + 1)
                if n >= 2:
                    pool.wait_ge(s_filled, S_NO["rowmaxT", (n - 2) // BLOCKS, (n - 2) % BLOCKS] + 1)
                k = b % 2
                part = [mparts[:, k, :, m, :] for m in range(MROWS)]
                whole, rest = (x[:, k, :].rearrange("p (h t) -> p h t", h=HG) for x in (negmax, mrest))
                link(nc.gpsimd.tensor_copy(part[0], whole))
                link(nc.gpsimd.tensor_tensor(out=rest, in0=whole, in1=part[0], op=ALU.subtract))
                link(nc.gpsimd.tensor_copy(part[1], rest))
                nc.gpsimd.tensor_tensor(out=part[2], in0=rest, in1=part[1],
                                        op=ALU.subtract).then_inc(mparts_ready, 1)

            def rotate_down(n):
                if n < DC:
                    if n == 0:
                        pool.wait_ge(wffn_in, 48)
                        pool.wait_ge(cols_ready, 1)
                        pool.wait_ge(v_proj, TILES // 2)
                    link(nc.gpsimd.tensor_scalar(wd_raw[:, n, :], wd_raw[:, n, :],
                                                 cols[:, C_WDP + n:C_WDP + n + 1],
                                                 float(INTER) ** -0.5, ALU.mult, ALU.mult))
                    return
                step, half = divmod(n - DC, 2)
                w = P << step
                a, o = (x.rearrange("p c (m two w) -> p (c m) two w", two=2, w=w)
                        for x in ((wd_raw, WDx[:, :, :]) if step % 2 == 0 else (WDx[:, :, :], wd_raw)))
                ins = nc.gpsimd.tensor_tensor(out=o[:, :, half, :], in0=a[:, :, 0, :], in1=a[:, :, 1, :],
                                              op=(ALU.add, ALU.subtract)[half])
                if n < DC + 5:
                    link(ins)
                else:
                    ins.then_inc(wd_rot, 1)

            rotation = [(0, b, j) for b in (1, 2) for j in range(TPB)]

            for s in ORDER:
                if s[0] == "rowmax":
                    split_max(*s[1:])
                elif s[0] == "exp" and s[1:4] in rotation and s[4] == 0:
                    rotate_down(rotation.index(s[1:4]))
                elif s[0] == "exp" and is_diag(s[2], s[3]) and s[4] == HG - EH:
                    _, g, b, j, _ = s
                    off = (j - TPB * b) * P
                    pool.wait_ge(t_read, t_done(g, b, j))
                    v = PR[:, unit_no(g, b, j) % PRING, :, off:off + P]
                    nc.gpsimd.affine_select(out=v, in_=v, compare_op=ALU.is_ge, fill=0.0, base=0,
                                            pattern=[[0, HG], [1, P]], channel_multiplier=-1)\
                        .then_inc(masked, 1)
                elif s[0] == "av" and s[2] == BLOCKS - 1 and s[3] % TPB == TPB - 1 and s[1] < GROUPS - 1:
                    pool.wait_ge(av_done, unit_no(*s[1:]) + 1)
                    load_vg(s[1] + 1, s[3] // TPB)
                elif s[0] == "norm" and s[1] == GROUPS - 1:
                    pool.wait_ge(xre_in, 16)
                    v = X1[:, s[2] * TPB:(s[2] + 1) * TPB, :]
                    nc.gpsimd.tensor_tensor(out=v, in0=v, in1=bo_all[:, :].unsqueeze(1)
                                            .to_broadcast([P, TPB, D]), op=ALU.add).then_inc(xb_ready, 1)
                elif s[0] == "oproj" and s[2]:
                    k = s[1] * TPB
                    pool.wait_ge(var2, s[1] + 1)
                    nc.gpsimd.tensor_tensor(out=rstd[:, k:k + TPB], in0=var_eps[:, k:k + TPB],
                                            in1=halves[:, k:k + TPB], op=ALU.pow).then_inc(rstd2, 1)

        @block.scalar
        def _(act):
            act.sem_inc(h_hi, START)
            act.wait_ge(wa_in, 48)
            nc.scalar.activation(WAh[:, :, :, :], wa_raw[:, :, :, :], ACT.Copy).then_inc(wa_hi, 1)
            act.wait_ge(cols_ready, 1)

            def norm_x(b):
                for c in range(DC):
                    n = b * DC + c
                    act.wait_ge(xT, n + 1)
                    if n >= 2:
                        act.wait_ge(xsplit, n - 1)
                    if b >= 2:
                        act.wait_ge(v_proj, 2 * (b - 1))
                    for dst in (xnf[:, n % 2, :], XTh[:, b % 2, c, :]):
                        nc.scalar.activation(dst, psS[:, n % 2, :], ACT.Identity,
                                             bias=cols[:, C_B + c:C_B + c + 1],
                                             scale=cols[:, C_G + c:C_G + c + 1]).then_inc(xnf_ready, 1)

            def part1(r):
                act.wait_ge(bank_read, r + 1)
                nc.scalar.activation(parts[:, r % PARTS, 1, :], part_rest[:, r % RESTS, :], ACT.Copy)\
                    .then_inc(rest_ready, 1)

            norm_x(0)
            for b in range(BLOCKS):
                for r in range(4 * b, 4 * b + 4):
                    if r % 4 == 2 and b + 1 < BLOCKS:
                        norm_x(b + 1)
                    _, w, half = QK_ROUNDS[r]
                    c = (C_BQ, C_BK)[w] + half
                    act.wait_ge(qk_proj, r + 1)
                    if r >= PARTS:
                        act.wait_ge(scr_out[r % PARTS], 16 * (r // PARTS))
                    nc.scalar.activation(parts[:, r % PARTS, 0, :], psT[:, r % 4, :], ACT.Identity,
                                         bias=cols[:, c:c + 1]).then_inc(part0, 1)
                    if r:
                        part1(r - 1)
            part1(len(QK_ROUNDS) - 1)

            def prep_out(n):
                q, bank = n % 4, psT[:, T_NO["prep", n] % TRING * EH, :]
                act.wait_ge(t_filled, T_NO["prep", n] + 1)
                if n < 16:
                    c = n // 4 % 2
                    dst, scale = (WT, float(D) ** -0.5) if n < 8 else \
                        (wug, cols[:, C_SUG + c:C_SUG + c + 1])
                    if n == 0:
                        act.wait_ge(v_proj, TILES // 2)
                    nc.scalar.activation(dst[:, c, q * BW:(q + 1) * BW], bank, ACT.Copy,
                                         scale=scale).then_inc(t_read, 1)
                elif n < 20:
                    nc.scalar.activation(WDT[:, 2 * q:2 * q + 2, :].rearrange("p c o -> p (c o)"),
                                         bank, ACT.Copy).then_inc(t_read, 1)
                else:
                    for j in range(2):
                        c = 2 * q + j
                        last = nc.scalar.activation(wd[:, c, :], bank[:, j * D:(j + 1) * D], ACT.Copy,
                                                    scale=cols[:, C_SDP + c:C_SDP + c + 1])
                    last.then_inc(t_read, 1)

            def weights_hi(k):
                act.wait_ge(av_done, GROUPS * UNITS)
                if k == "down":
                    last = nc.scalar.activation(Dh[:, :, :], wd, ACT.Copy)
                else:
                    for c in range(DC):
                        last = nc.scalar.activation(ug_chunk(UGh, c, k), ug_chunk(wug, c, k), ACT.Copy)
                last.then_inc(wsplit_hi, 1)

            def ffn_chunk(b, k):
                act.wait_ge(ug_mm, b * IC + k + 1)
                if not at_start(b, k, 2):
                    act.wait_ge(h_ready, b * IC + k - 1 + START)
                nc.scalar.activation(sg[:, k % 2, :], psT[:, 2 * (k % 2), :], ACT.Silu,
                                     scale=cols[:, C_WUG + IC + k:C_WUG + IC + k + 1]).then_inc(silu_ready, 1)
                act.wait_ge(h_ready, b * IC + k + 1 + START)
                if not at_start(b, k, 4):
                    act.wait_ge(down_k, b * IC + k - 3 + START)
                nc.scalar.activation(Hh[:, k % 4, :], hf[:, k % 2, :], ACT.Copy).then_inc(h_hi, 1)

            def hi_from_psum(s, done, dst, where):
                act.wait_ge(s_filled, S_NO[s] + 1)
                nc.scalar.activation(dst[:, s[2], where], psS[:, S_BANK[S_NO[s]], :], ACT.Copy)\
                    .then_inc(done, 1)

            for s in ORDER:
                if s[0] == "prep":
                    prep_out(s[1])
                elif s[0] == "wsplit":
                    weights_hi(s[1])
                elif s[0] == "ug":
                    ffn_chunk(0, s[1])
                elif s[0] == "exp":
                    _, g, b, j, h = s
                    u = unit_no(g, b, j)
                    off = max(j - TPB * b, 0) * P
                    slot = T_NO[s] % TRING * EH
                    act.wait_ge(t_filled, T_NO[s] + 1)
                    if u + h == 0:
                        for i in range(PARTS):
                            act.wait_ge(scr_out[i], 16 * len(QK_ROUNDS[i::PARTS]))
                    if h == 0 and u >= PRING:
                        act.wait_ge(av_done, u + 1 - PRING)
                    nc.scalar.activation(PR[:, u % PRING, h:h + EH, off:BW], psT[:, slot:slot + EH, off:BW],
                                         ACT.Exp, scale=float(DH) ** -0.5).then_inc(t_read, 1)
                elif s[0] == "avout":
                    _, g, b = s
                    n = g * BLOCKS + b
                    act.wait_ge(av_done, unit_no(g, b, TPB * (b + 1) - 1) + 1)
                    if n >= 2:
                        act.wait_ge(s_filled, S_NO["norm", (n - 2) // BLOCKS, (n - 2) % BLOCKS] + 1)
                    nc.scalar.activation(avT[:, b % 2, :], psA[:, :], ACT.Copy).then_inc(av_out, 1)
                elif s[0] == "norm" and s[1:] == (GROUPS - 1, 0):
                    act.wait_ge(wo_in, 16)
                    nc.scalar.activation(Woh[:, :, :], wo_raw[:, :, :], ACT.Copy).then_inc(wsplit_hi, 1)
                elif s[0] == "oT":
                    hi_from_psum(s, oT_hi, OTh, slice(0, BW))
                elif s[0] == "x2T":
                    hi_from_psum(s, x2_hi, X2h, slice(s[1] * BW, (s[1] + 1) * BW))

            with act.Fori(1, BLOCKS) as b:
                for k in range(IC):
                    ffn_chunk(b, k)

        @block.vector
        def _(dve):
            for s in (h_ready, y_ready):
                dve.sem_inc(s, START)
            chain = [0]

            def link(ins):
                chain[0] += 1
                ins.then_inc(dve_link, 1)
                dve.wait_ge(dve_link, chain[0])

            def x_stats(b):
                ts = range(b * TPB, (b + 1) * TPB)
                dve.wait_ge(x_in[b], 16)
                for t in ts:
                    last = nc.vector.bn_stats(stats[:, t, :], xin[:, t, :])
                link(last)
                for t in ts:
                    last = nc.vector.bn_aggr(meanvar[:, t, :], stats[:, t, :])
                link(last)
                nc.vector.tensor_scalar(var_eps[:, ts.start:ts.stop], meanvar[:, ts.start:ts.stop, 1],
                                        1.0 + EPS, EPS * EPS, ALU.mult, ALU.add).then_inc(var_ready, 1)

            def x_shift(b):
                ts = slice(b * TPB, (b + 1) * TPB)
                dve.wait_ge(rstd_ready, b + 1)
                link(nc.vector.scalar_tensor_tensor(out=lnshift[:, ts], in0=meanvar[:, ts, 0], scalar=-1.0,
                                                    in1=rstd[:, ts], op0=ALU.mult, op1=ALU.mult))

            def scale_x(b):
                for t in range(b * TPB, (b + 1) * TPB):
                    nc.vector.tensor_scalar(xin[:, t, :], xin[:, t, :], rstd[:, t:t + 1],
                                            lnshift[:, t:t + 1], ALU.mult, ALU.add).then_inc(xh_ready, 1)

            def split_x(b):
                for c in range(DC):
                    n = b * DC + c
                    dve.wait_ge(xnf_ready, 2 * n + 2)
                    nc.vector.tensor_tensor(out=XTl[:, b % 2, c, :], in0=xnf[:, n % 2, :],
                                            in1=XTh[:, b % 2, c, :].bitcast(f32),
                                            op=ALU.subtract).then_inc(xsplit, 1)

            x_stats(0)
            x_shift(0)
            scale_x(0)
            dve.wait_ge(rowsT, 1)
            nc.vector.tensor_copy(cols[:, :], psM[:, 0:NCOLS]).then_inc(cols_ready, 1)
            dve.wait_ge(wa_hi, 1)
            nc.vector.tensor_tensor(out=WAl[:, :, :, :], in0=wa_raw[:, :, :, :],
                                    in1=WAh[:, :, :, :].bitcast(f32), op=ALU.subtract).then_inc(wa_split, 1)
            x_stats(1)
            split_x(0)
            dve.wait_ge(bias_in, 32)
            for b in range(BLOCKS):
                if b + 1 < BLOCKS:
                    x_shift(b + 1)
                    scale_x(b + 1)
                if b + 2 < BLOCKS:
                    x_stats(b + 2)
                for r in range(4 * b, 4 * b + 4):
                    if r % 4 == 2 and b + 1 < BLOCKS:
                        split_x(b + 1)
                    _, w, half = QK_ROUNDS[r]
                    c = (C_BQ, C_BK)[w] + half
                    dve.wait_ge(part0, r + 1)
                    if r >= RESTS:
                        dve.wait_ge(parts_ready, r - RESTS + 1)
                    nc.vector.scalar_tensor_tensor(out=part_rest[:, r % RESTS, :], in0=psT[:, r % 4, :],
                                                   scalar=cols[:, c:c + 1], in1=parts[:, r % PARTS, 0, :],
                                                   op0=ALU.add, op1=ALU.subtract).then_inc(bank_read, 1)
                for v in range(2 * b, 2 * b + 2):
                    dve.wait_ge(v_proj, v + 1)
                    bank = (psA, psM)[v % 2]
                    nc.vector.tensor_tensor(out=V[:, 2 * v:2 * v + 2, :],
                                            in0=bank[:, :].rearrange("p (t n) -> p t n", t=2),
                                            in1=bv_all[:, :].unsqueeze(1).to_broadcast([P, 2, D]),
                                            op=ALU.add).then_inc(v_ready, 1)

            dve.wait_ge(consts_ready, 6)

            def reduce_bank(s):
                _, g, i, k = s
                _, heads, _, width, slot = max_jobs(i)[k]
                dve.wait_ge(s_filled, S_NO[s] + 1)
                nc.vector.tensor_reduce(pmax[:, (i // TPB) % 2, i % TPB, heads[0]:heads[-1] + 1, slot],
                                        psS[:, S_BANK[S_NO[s]], 0:len(heads) * width]
                                        .rearrange("p (h n) -> p h n", n=width),
                                        axis=AX.X, op=ALU.max).then_inc(s_read, 1)

            def block_max(g, b):
                n = g * BLOCKS + b
                dve.wait_ge(s_read, S_NO["max", g, b * TPB + TPB - 1, len(max_jobs(b * TPB + TPB - 1)) - 1] + 1)
                if n >= 2:
                    dve.wait_ge(mparts_ready, n - 1)
                nc.vector.tensor_reduce(negmax[:, b % 2, :].rearrange("p (h t) -> p t h", t=TPB),
                                        pmax[:, b % 2, :, :, 0:2 + b],
                                        axis=AX.X, op=ALU.max, negate=True).then_inc(rowmax_ready, 1)

            def max_rows(s):
                _, g, b = s
                n = g * BLOCKS + b
                dve.wait_ge(s_filled, S_NO[s] + 1)
                if n >= 2:
                    dve.wait_ge(mrows_in[b % 2], n // 2 * (16 * HG))
                nc.vector.tensor_copy(mrows[:, b % 2, :],
                                      psS[:, S_BANK[S_NO[s]], :].bitcast(bf16)[0:MROWS * HG * TPB, 0:P])\
                    .then_inc(mrows_ready, 1)
                dve.wait_ge(mrows_ready, n + 1)
                dve.sem_inc(s_read, 1)

            def normalise(s):
                _, g, b = s
                dve.wait_ge(s_filled, S_NO[s] + 1)
                v = psS[:, S_BANK[S_NO[s]], :].rearrange("p (t h n) -> p t h n", t=TPB, h=HG)
                nc.vector.reciprocal(recip[:, b % 2, :].rearrange("p (t h) -> p t h", t=TPB),
                                     v[:, :, :, DH]).then_inc(recip_ready, 1)
                dve.wait_ge(recip_ready, g * BLOCKS + b + 1)
                o = O[:, b * TPB:(b + 1) * TPB, g * HG * DH:(g + 1) * HG * DH]\
                    .rearrange("p t (h d) -> p t h d", d=DH)
                r = recip[:, b % 2, :].rearrange("p (t h) -> p t h", t=TPB)\
                    .unsqueeze(3).to_broadcast([P, TPB, HG, DH])
                nc.vector.tensor_tensor(out=o, in0=v[:, :, :, 0:DH], in1=r, op=ALU.mult).then_inc(s_read, 1)

            def lo_from_psum(s, hi_done, dst, hi, where):
                _, b, c = s
                dve.wait_ge(hi_done, b * DC + c + 1)
                nc.vector.tensor_tensor(out=dst[:, c, where], in0=psS[:, S_BANK[S_NO[s]], :],
                                        in1=hi[:, c, where].bitcast(f32), op=ALU.subtract).then_inc(s_read, 1)

            def residual(s):
                _, b, v = s
                if v == 0:
                    dve.wait_ge(xb_ready, b + 1)
                dve.wait_ge(s_filled, S_NO[s] + 1)
                t = b * TPB + 2 * v
                nc.vector.tensor_tensor(out=X1[:, t:t + 2, :],
                                        in0=psS[:, S_BANK[S_NO[s]], :].rearrange("p (t n) -> p t n", t=2),
                                        in1=X1[:, t:t + 2, :], op=ALU.add).then_inc(s_read, 1)
                dve.wait_ge(s_read, S_NO[s] + 1)
                for x in range(t, t + 2):
                    last = nc.vector.bn_stats(stats[:, x, :], X1[:, x, :])
                if v == 0:
                    return
                link(last)
                k = b * TPB
                for x in range(k, k + TPB):
                    last = nc.vector.bn_aggr(meanvar[:, x, :], stats[:, x, :])
                link(last)
                nc.vector.tensor_scalar(var_eps[:, k:k + TPB], meanvar[:, k:k + TPB, 1], EPS, None,
                                        ALU.add).then_inc(var2, 1)

            def norm2(b):
                k = b * TPB
                dve.wait_ge(rstd2, b + 1)
                link(nc.vector.scalar_tensor_tensor(out=lnshift[:, k:k + TPB], in0=meanvar[:, k:k + TPB, 0],
                                                    scalar=-1.0, in1=rstd[:, k:k + TPB],
                                                    op0=ALU.mult, op1=ALU.mult))
                if b >= 1:
                    dve.wait_ge(s_filled, S_NO["x2T", b - 1, DC - 1] + 1)
                for t in range(TPB):
                    last = nc.vector.tensor_scalar(xh2[:, t, :], X1[:, k + t, :],
                                                   rstd[:, k + t:k + t + 1], lnshift[:, k + t:k + t + 1],
                                                   ALU.mult, ALU.add)
                last.then_inc(xh2_ready, 1)

            def weights_lo(k):
                dve.wait_ge(wsplit_hi, W_NO[k] + 1)
                if k == "down":
                    last = nc.vector.tensor_tensor(out=Dl[:, :, :], in0=wd, in1=Dh[:, :, :].bitcast(f32),
                                                   op=ALU.subtract)
                else:
                    for c in range(DC):
                        last = nc.vector.tensor_tensor(out=ug_chunk(UGl, c, k), in0=ug_chunk(wug, c, k),
                                                       in1=ug_chunk(UGh, c, k).bitcast(f32), op=ALU.subtract)
                last.then_inc(wsplit, 1)

            def ffn_chunk(b, k):
                dve.wait_ge(silu_ready, b * IC + k + 1)
                if not at_start(b, k, 2):
                    dve.wait_ge(h_hi, b * IC + k - 1 + START)
                nc.vector.scalar_tensor_tensor(out=hf[:, k % 2, :], in0=psT[:, 2 * (k % 2) + 1, :],
                                               scalar=cols[:, C_WUG + k:C_WUG + k + 1], in1=sg[:, k % 2, :],
                                               op0=ALU.mult, op1=ALU.mult).then_inc(h_ready, 1)
                dve.wait_ge(h_hi, b * IC + k + 1 + START)
                nc.vector.tensor_tensor(out=Hl[:, k % 4, :], in0=hf[:, k % 2, :],
                                        in1=Hh[:, k % 4, :].bitcast(f32), op=ALU.subtract).then_inc(h_split, 1)

            def ffn_out(b):
                dve.wait_ge(y_out, b * 16 + START)
                dve.wait_ge(down_k, b * IC + IC + START)
                for v, bank in enumerate((psA, psM)):
                    nc.vector.tensor_tensor(out=yst[:, 2 * v:2 * v + 2, :],
                                            in0=bank[:, :].rearrange("p (t n) -> p t n", t=2),
                                            in1=X1[:, ds(b * TPB + 2 * v, 2), :],
                                            op=ALU.add).then_inc(y_ready, 1)

            for s in ORDER:
                if s[0] == "max":
                    reduce_bank(s)
                elif s[0] == "wsplit":
                    weights_lo(s[1])
                elif s[0] == "ug":
                    ffn_chunk(0, s[1])
                elif s[0] == "rowmax":
                    block_max(*s[1:])
                elif s[0] == "rowmaxT":
                    max_rows(s)
                elif s[0] == "norm":
                    normalise(s)
                    if s[1:] == (GROUPS - 1, 0):
                        dve.wait_ge(wsplit_hi, 1)
                        nc.vector.tensor_tensor(out=Wol[:, :, :], in0=wo_raw[:, :, :],
                                                in1=Woh[:, :, :].bitcast(f32),
                                                op=ALU.subtract).then_inc(wsplit, 1)
                elif s[0] == "oT":
                    lo_from_psum(s, oT_hi, OTl, OTh, slice(0, BW))
                elif s[0] == "oproj":
                    residual(s)
                elif s[0] == "xh2":
                    norm2(s[1])
                elif s[0] == "x2T":
                    lo_from_psum(s, x2_hi, X2l, X2h, slice(s[1] * BW, (s[1] + 1) * BW))

            with dve.Fori(1, BLOCKS) as b:
                for k in range(IC):
                    ffn_chunk(b, k)
                    if k == 1:
                        ffn_out(b - 1)
            ffn_out(LAST)

        @block.tensor
        def _(pe):
            pe.sem_inc(down_k, START)
            pe.wait_ge(consts_ready, 4)

            def transpose_x(b):
                pe.wait_ge(xh_ready, TPB * (b + 1))
                for c in range(DC):
                    n = b * DC + c
                    if n >= 2:
                        pe.wait_ge(xnf_ready, 2 * n - 2)
                    for t in range(TPB):
                        last = nc.tensor.transpose(psS[:, n % 2, t * P:(t + 1) * P],
                                                   xin[:, b * TPB + t, c * P:(c + 1) * P], identf[:, :])
                    last.then_inc(xT, 1)

            def hilo(bank, lh, ll, rh, rl):
                n = len(lh)
                for c in range(n):
                    for m, (a, x) in enumerate(((lh[c], rh[c]), (lh[c], rl[c]), (ll[c], rh[c]))):
                        last = nc.tensor.matmul(bank, a, x, start=(c == 0 and m == 0),
                                                stop=(c == n - 1 and m == 2))
                return last

            pe.wait_ge(rows_in, 16 * 8)
            nc.tensor.transpose(psM[:, 0:NCOLS], rows[:, :], identf[0:NCOLS, 0:NCOLS]).then_inc(rowsT, 1)
            transpose_x(0)
            pe.wait_ge(wa_split, 1)
            for b in range(BLOCKS):
                pe.wait_ge(xsplit, DC * (b + 1))
                xh = [XTh[:, b % 2, c, :] for c in range(DC)]
                xl = [XTl[:, b % 2, c, :] for c in range(DC)]
                for r in range(4 * b, 4 * b + 4):
                    if r % 4 == 2 and b + 1 < BLOCKS:
                        transpose_x(b + 1)
                    _, w, half = QK_ROUNDS[r]
                    f = slice(half * P, (half + 1) * P)
                    if r >= 4:
                        pe.wait_ge(bank_read, r - 3)
                    hilo(psT[:, r % 4, :], [WAh[:, w, c, f] for c in range(DC)],
                         [WAl[:, w, c, f] for c in range(DC)], xh, xl).then_inc(qk_proj, 1)
                for v in range(2 * b, 2 * b + 2):
                    if v >= 2:
                        pe.wait_ge(v_ready, v - 1)
                    if v == 1:
                        pe.wait_ge(cols_ready, 1)
                    for t in range(2):
                        k = slice(((2 * v + t) % TPB) * P, ((2 * v + t) % TPB + 1) * P)
                        last = hilo((psA, psM)[v % 2][:, t * D:(t + 1) * D],
                                    [XTh[:, b % 2, c, k] for c in range(DC)],
                                    [XTl[:, b % 2, c, k] for c in range(DC)],
                                    [WAh[:, 2, c, :] for c in range(DC)],
                                    [WAl[:, 2, c, :] for c in range(DC)])
                    last.then_inc(v_proj, 1)

            def prep(n):
                q, bank = n % 4, psT[:, T_NO["prep", n] % TRING * EH, :]
                t_slot("prep", n)
                if n < 8:
                    if n == 0:
                        pe.wait_ge(wffn_in, 48)
                    c = n // 4
                    for t in range(4):
                        last = nc.tensor.transpose(bank[:, t * P:(t + 1) * P],
                                                   wug_raw[:, 4 * q + t, c * P:(c + 1) * P], identf[:, :])
                elif n < 16:
                    c = (n - 8) // 4
                    if n == 8:
                        pe.wait_ge(hadm_ready, 1)
                        pe.wait_ge(t_read, T_NO["prep", 7] + 1)
                    nc.tensor.matmul(bank, hadp[:, :], WT[:, 0, q * BW:(q + 1) * BW],
                                     start=True, stop=False)
                    last = nc.tensor.matmul(bank, (hadp, hadm)[c][:, :],
                                            WT[:, 1, q * BW:(q + 1) * BW], start=False, stop=True)
                elif n < 20:
                    if n == 16:
                        pe.wait_ge(wd_rot, 1)
                    for j in range(2):
                        for c in range(DC):
                            k = 2 * q + j
                            last = nc.tensor.transpose(bank[:, j * D + c * P:j * D + (c + 1) * P],
                                                       WDx[:, c, k * P:(k + 1) * P], identf[:, :])
                else:
                    pe.wait_ge(t_read, T_NO["prep", n - 4] + 1)
                    last = nc.tensor.matmul(bank, hadp[:, :],
                                            WDT[:, 2 * q:2 * q + 2, :].rearrange("p c o -> p (c o)"),
                                            start=True, stop=True)
                last.then_inc(t_filled, 1)

            def t_slot(*s):
                if T_NO[s] == 0:
                    pe.wait_ge(bank_read, len(QK_ROUNDS))
                if T_NO[s] >= TRING:
                    pe.wait_ge(t_read, T_NO[s] - TRING + 1)

            def s_bank(s):
                if S_NO[s] == SRING - 1:
                    pe.wait_ge(v_ready, TILES // 2)
                if S_PREV[S_NO[s]] is not None:
                    pe.wait_ge(s_read, S_PREV[S_NO[s]] + 1)
                return psS[:, S_BANK[S_NO[s]], :]

            def max_scores(s):
                _, g, i, k = s
                kind, heads, k0, width, _ = max_jobs(i)[k]
                if g == 0 and k == 0 and i % TPB == 0:
                    pe.wait_ge(ops0_in[i // TPB], 16 * 2 * SLOTS)
                elif i == 0 and k == 0:
                    pe.wait_ge(ops_in, g * (16 * 2 * SLOTS))
                bank = s_bank(s)
                if kind == "diag":
                    nc.tensor.matmul(bank, identb[:, :], mask[:, :, :], start=True, stop=False)
                for m, h in enumerate(heads):
                    last = nc.tensor.matmul(bank[:, m * width:(m + 1) * width],
                                            QA[0:ROWS, g % 2, h, i * P:(i + 1) * P],
                                            KA[0:ROWS, g % 2, h, k0:k0 + width],
                                            start=(kind != "diag"),
                                            stop=(kind != "diag" or m == len(heads) - 1))
                last.then_inc(s_filled, 1)

            def exp_scores(s):
                _, g, b, j, h = s
                off = max(j - TPB * b, 0) * P
                t_slot(*s)
                if j == 0 and h == 0:
                    pe.wait_ge(mrows_in[b % 2], ((g * BLOCKS + b) // 2 + 1) * (16 * HG))
                for m in range(EH):
                    last = nc.tensor.matmul(
                        psT[:, T_NO[s] % TRING * EH + m, off:BW],
                        KA[0:ROWS + MROWS, g % 2, h + m, j * P:(j + 1) * P],
                        QA[0:ROWS + MROWS, g % 2, h + m, b * BW + off:(b + 1) * BW],
                        start=True, stop=True)
                last.then_inc(t_filled, 1)

            def product_v(g, b, j):
                off = max(j - TPB * b, 0) * P
                if is_diag(b, j):
                    pe.wait_ge(masked, diag_no(g, b, j))
                else:
                    pe.wait_ge(t_read, t_done(g, b, j))
                if j == 0 and g + b:
                    pe.wait_ge(av_out, g * BLOCKS + b)
                if j == TPB * b:
                    pe.wait_ge(vg_ready, g * BLOCKS + b + 1)
                for h in range(HG):
                    last = nc.tensor.matmul(psA[32 * h:32 * h + 32, off:BW], VG[:, j, h, :],
                                            PR[:, unit_no(g, b, j) % PRING, h, off:BW],
                                            start=(j == 0), stop=(j == TPB * (b + 1) - 1))
                last.then_inc(av_done, 1)

            def transposes(s, rows_of, c):
                bank = s_bank(s)
                for t in range(TPB):
                    last = nc.tensor.transpose(bank[:, t * P:(t + 1) * P],
                                               rows_of(t)[:, c * P:(c + 1) * P], identf[:, :])
                last.then_inc(s_filled, 1)

            def up_gate(b, k):
                if not at_start(b, k, 2):
                    pe.wait_ge(h_ready, b * IC + k - 1 + START)
                for which in range(2):
                    f = slice((1 - which) * INTER + k * P, (1 - which) * INTER + (k + 1) * P)
                    xs = ds(b * BW, BW)
                    last = hilo(psT[:, 2 * (k % 2) + which, :],
                                [UGh[:, c, f] for c in range(DC)], [UGl[:, c, f] for c in range(DC)],
                                [X2h[:, c, xs] for c in range(DC)], [X2l[:, c, xs] for c in range(DC)])
                last.then_inc(ug_mm, 1)

            def down(b, k):
                pe.wait_ge(h_split, b * IC + k + 1)
                if k == 0:
                    pe.wait_ge(y_ready, b * 2 + START)
                    for bank in (psA, psM):
                        nc.tensor.matmul(bank[:, :], zerob[:, :], mask[:, :, :], start=True, stop=False)
                for t in range(TPB):
                    sl = slice(t * P, (t + 1) * P)
                    for m, (a, x) in enumerate(((Hh, Dh), (Hh, Dl), (Hl, Dh))):
                        last = nc.tensor.matmul(down_bank(t), a[:, k % 4, sl], x[:, k, :], start=False,
                                                stop=(k == IC - 1 and m == 2 and t % 2 == 1))
                last.then_inc(down_k, 1)

            pe.wait_ge(consts_ready, 6)
            first_exp = True
            for s in ORDER:
                if s[0] == "max":
                    max_scores(s)
                elif s[0] == "rowmaxT":
                    _, g, b = s
                    pe.wait_ge(mparts_ready, g * BLOCKS + b + 1)
                    nc.tensor.transpose(s_bank(s).bitcast(bf16)[0:MROWS * HG * TPB, 0:P],
                                        mparts[:, b % 2, :, :, :].rearrange("p h m t -> p (h m t)"),
                                        identb[:, :]).then_inc(s_filled, 1)
                elif s[0] == "prep":
                    prep(s[1])
                elif s[0] == "exp":
                    if first_exp:
                        pe.wait_ge(ones_in, 16 * 2 * HG)
                        first_exp = False
                    exp_scores(s)
                elif s[0] == "av":
                    product_v(*s[1:])
                elif s[0] == "norm":
                    _, g, b = s
                    bank = s_bank(s)
                    pe.wait_ge(av_out, g * BLOCKS + b + 1)
                    for t in range(TPB):
                        last = nc.tensor.transpose(bank[:, t * P:(t + 1) * P],
                                                   avT[:, b % 2, t * P:(t + 1) * P], identf[:, :])
                    last.then_inc(s_filled, 1)
                elif s[0] == "oT":
                    _, b, c = s
                    pe.wait_ge(s_read, S_NO["norm", GROUPS - 1, b] + 1)
                    transposes(s, lambda t: O[:, b * TPB + t, :], c)
                elif s[0] == "oproj":
                    _, b, v = s
                    pe.wait_ge(s_read, S_NO["oT", b, DC - 1] + 1)
                    pe.wait_ge(wsplit, 1)
                    bank = s_bank(s)
                    for t in range(2):
                        k = slice((2 * v + t) * P, (2 * v + t + 1) * P)
                        last = hilo(bank[:, t * D:(t + 1) * D],
                                    [OTh[:, c, k] for c in range(DC)], [OTl[:, c, k] for c in range(DC)],
                                    [Woh[:, c, :] for c in range(DC)], [Wol[:, c, :] for c in range(DC)])
                    last.then_inc(s_filled, 1)
                elif s[0] == "ug":
                    if s[1] == 0:
                        pe.wait_ge(s_read, S_NO["x2T", 0, DC - 1] + 1)
                        pe.wait_ge(t_read, len(T_STEPS))
                    pe.wait_ge(wsplit, W_NO[s[1]] + 1)
                    up_gate(0, s[1])
                elif s[0] == "down":
                    if s[1] == 0:
                        pe.wait_ge(wsplit, W_NO["down"] + 1)
                        pe.wait_ge(av_out, GROUPS * BLOCKS)
                        pe.wait_ge(s_read, max(n for n, x in enumerate(S_BANK) if x == SRING - 1) + 1)
                    down(0, s[1])
                elif s[0] == "x2T":
                    pe.wait_ge(xh2_ready, s[1] + 1)
                    transposes(s, lambda t: xh2[:, t, :], s[2])
            pe.wait_ge(s_read, len(S_STEPS))

            with pe.Fori(1, BLOCKS) as b:
                for k in range(IC):
                    up_gate(b, k)
                    if k < 2:
                        down(b - 1, IC - 2 + k)
                    elif k == 3:
                        down(b, 0)
                        down(b, 1)
                    elif k > 3:
                        down(b, k - 2)
            down(LAST, IC - 2)
            down(LAST, IC - 1)


_INS = ["L0_attn_X", "L0_attn_ln_g", "L0_attn_ln_b", "L0_attn_Wq", "L0_attn_bq", "L0_attn_Wk",
        "L0_attn_bk", "L0_attn_Wv", "L0_attn_bv", "L0_attn_Wo", "L0_attn_bo", "L0_ffn_SU_ug",
        "L0_ffn_SU_dp", "L0_ffn_Wscale_ug", "L0_ffn_Wscale_dp", "L0_ffn_W_up", "L0_ffn_W_gate",
        "L0_ffn_W_down"]


def kernel(**inputs):
    import numpy as np
    import concourse.bacc as bacc
    from concourse.bass_utils import run_bass_kernel_spmd

    nc = bacc.Bacc("TRN2", target_bir_lowering=False, num_devices=1)
    arrays, args = {}, []
    for name in _INS:
        a = np.ascontiguousarray(inputs[name])
        arrays[name] = a
        args.append(nc.dram_tensor(name, a.shape, mybir.dt.from_np(a.dtype), kind="ExternalInput").ap())
    had = np.ones((1, 1), np.float32)
    while had.shape[0] < P:
        had = np.block([[had, had], [had, -had]])
    arrays["had"] = np.ascontiguousarray(had, np.float32)
    args.append(nc.dram_tensor("had", (P, P), mybir.dt.float32, kind="ExternalInput").ap())
    args.append(nc.dram_tensor("out", (1, SEQ, D), mybir.dt.float32, kind="ExternalOutput").ap())
    build(nc, *args)
    r = run_bass_kernel_spmd(nc, [arrays], core_ids=[0])
    return r.results[0]["out"]
```
